# Optimizing a Trainium2 kernel written in Bass

```python
import numpy as np
import jax
import jax.numpy as jnp

def _softmax(x, axis=-1):
    return jax.nn.softmax(x, axis=axis)

def _gelu(x):
    return jax.nn.gelu(x, approximate=True)

def _silu(x):
    return jax.nn.silu(x)

def _sigmoid(x):
    return jax.nn.sigmoid(x)

def _layernorm(x, axis=-1, eps=1e-05):
    m = jnp.mean(x, axis=axis, keepdims=True)
    v = jnp.var(x, axis=axis, keepdims=True)
    return (x - m) / jnp.sqrt(v + eps)

def _scatter_add(tgt, idx, src, axis=0):
    return tgt.at[idx].add(src)

def _segment_sum(src, seg, n):
    return jax.ops.segment_sum(src, seg, n)
kernel_name = 'mk_cond_resid_d4_seqx_r4_87040c'

def setup_inputs(seed: int=0):
    np.random.seed(seed)
    _w = jnp.asarray

    def _rec_inputs():
        import jax
        import jax.numpy as jnp
        _rk = jax.random.key(seed)
        x = -0.000125 + 0.9999 * jax.random.normal(jax.random.fold_in(_rk, 1), (32, 64, 1024), jnp.float32)
        _lenS = 64 - jax.random.randint(jax.random.fold_in(_rk, 7), (32,), 0, max(1, 64 // 4) + 1, jnp.int32)
        _lenS2 = 64 - jax.random.randint(jax.random.fold_in(_rk, 8), (32,), 0, max(1, 64 // 4) + 1, jnp.int32)
        itok_B_0_2 = jax.random.randint(jax.random.fold_in(_rk, 11), (32,), 0, 3, jnp.int32)
        itok_B_0_15 = jax.random.randint(jax.random.fold_in(_rk, 12), (32,), 0, 16, jnp.int32)
        itok_B_0_7 = jax.random.randint(jax.random.fold_in(_rk, 13), (32,), 0, 8, jnp.int32)
        condB_coeff = 0.00219231 + 0.0100837 * jax.random.normal(jax.random.fold_in(_rk, 14), (32,), jnp.float32)
        _validS = jnp.arange(64)[None, :] < _lenS[:, None]
        _validS2 = jnp.arange(64)[None, :] < _lenS2[:, None]
        _causal = jnp.tril(jnp.ones((64, 64), dtype=bool))
        mask_Bx4096x4096_ik1 = jnp.where(jnp.ones((32, 1024, 1024), dtype=bool), 1, 0).astype(jnp.int32)
        return (x, itok_B_0_2, itok_B_0_15, itok_B_0_7, condB_coeff, mask_Bx4096x4096_ik1)
    x, itok_B_0_2, itok_B_0_15, itok_B_0_7, condB_coeff, mask_Bx4096x4096_ik1 = _rec_inputs()

    def _L0_cond_setup():
        import jax, jax.numpy as jnp
        import numpy as np
        B, S, D_IN, D_OUT = (4, 512, 1024, 1024)
        R, NUM_LABELERS = (32, 5)
        LORA_SCALING = 16 / 32
        key = jax.random.key(seed)
        k1, k2, k3, k4, k5 = jax.random.split(key, 5)
        x = jax.random.normal(k1, (B, S, D_IN), dtype=jnp.float32)
        labeler_index = jax.random.randint(k2, (B,), 0, NUM_LABELERS, dtype=jnp.int64)
        W = jax.random.normal(k3, (D_OUT, D_IN), dtype=jnp.float32) * 0.02
        lora_A = jax.random.normal(k4, (NUM_LABELERS, D_IN, R), dtype=jnp.float32) * 0.02
        lora_B_w = jax.random.normal(k5, (D_OUT, R), dtype=jnp.float32) * 0.02
        return {'x': x, 'labeler_index': labeler_index, 'W': W, 'lora_A': lora_A, 'lora_B_w': lora_B_w}
    _L0_cond_all = _L0_cond_setup()
    _L0_cond_in = {k: v for k, v in _L0_cond_all.items() if k in ('W', 'lora_A', 'lora_B_w')}
    del _L0_cond_all

    def _L1_cond_setup():
        import jax, jax.numpy as jnp
        import numpy as np
        NUM_CONDITIONS = 16
        IN_CH = 64
        OUT_CH = 64
        B = 64
        T = 1024
        key = jax.random.key(seed)
        k_x, k_w, k_c = jax.random.split(key, 3)
        x = jax.random.normal(k_x, (B, IN_CH, T), dtype=jnp.float32)
        bound = float(np.sqrt(6.0 / IN_CH))
        weights = jax.random.uniform(k_w, (NUM_CONDITIONS, IN_CH, OUT_CH), dtype=jnp.float32, minval=-bound, maxval=bound)
        condition = jax.random.randint(k_c, (B,), 0, NUM_CONDITIONS, dtype=jnp.int64)
        return {'x': x, 'weights': weights, 'condition': condition}
    _L1_cond_all = _L1_cond_setup()
    _L1_cond_in = {k: v for k, v in _L1_cond_all.items() if k in ('weights',)}
    del _L1_cond_all

    def _L2_cond_setup():
        import jax, jax.numpy as jnp
        import numpy as np
        TOP_K = 2
        LANG_BIAS = 5.0
        SCALING = 32.0 / 16.0
        LANGUAGE_PAD_ID = -1
        key = jax.random.key(seed)
        ks = jax.random.split(key, 6)
        B, T, D, O, E, R = (4, 512, 1024, 1024, 8, 16)
        x = jax.random.normal(ks[0], (B, T, D), dtype=jnp.float32)
        language_ids = jax.random.randint(ks[1], (B,), 0, E).astype(jnp.int64)
        W = jax.random.normal(ks[2], (O, D), dtype=jnp.float32) * (1.0 / np.sqrt(D))
        Wr = jax.random.normal(ks[3], (E, D), dtype=jnp.float32) * (1.0 / np.sqrt(D))
        A = jax.random.normal(ks[4], (E, R, D), dtype=jnp.float32) * (1.0 / np.sqrt(D))
        Bm = jax.random.normal(ks[5], (O, R), dtype=jnp.float32) * 0.0
        Bm = jnp.broadcast_to(Bm, (E, O, R)) + jax.random.normal(ks[5], (E, O, R), dtype=jnp.float32) * 0.02
        return {'x': x, 'language_ids': language_ids, 'W': W, 'Wr': Wr, 'A': A, 'B': Bm}
    _L2_cond_all = _L2_cond_setup()
    _L2_cond_in = {k: v for k, v in _L2_cond_all.items() if k in ('W', 'Wr', 'A', 'B')}
    del _L2_cond_all

    def _L3_cond_setup():
        import jax, jax.numpy as jnp
        import numpy as np
        B, S, D_IN, D_OUT = (4, 128, 1024, 1024)
        key = jax.random.key(seed)
        k1, k2, k3, k4, k5 = jax.random.split(key, 5)
        hidden_states = jax.random.normal(k1, (B, S, D_IN), dtype=jnp.float32)
        W = jax.random.normal(k2, (D_OUT, D_IN), dtype=jnp.float32) * 0.02
        b = jax.random.normal(k3, (D_OUT,), dtype=jnp.float32) * 0.02
        coeff = jax.random.normal(k4, (B,), dtype=jnp.float32) * 0.01
        mask = jax.random.randint(k5, (B, D_IN, D_OUT), 0, 2, dtype=jnp.int32)
        return {'hidden_states': hidden_states, 'W': W, 'b': b, 'coeff': coeff, 'mask': mask}
    _L3_cond_all = _L3_cond_setup()
    _L3_cond_in = {k: v for k, v in _L3_cond_all.items() if k in ('W', 'b')}
    del _L3_cond_all
    return {'x': x, 'itok_B_0_2': itok_B_0_2, 'itok_B_0_15': itok_B_0_15, 'itok_B_0_7': itok_B_0_7, 'condB_coeff': condB_coeff, 'mask_Bx4096x4096_ik1': mask_Bx4096x4096_ik1, 'L0_cond_W': _L0_cond_in['W'], 'L0_cond_lora_A': _L0_cond_in['lora_A'], 'L0_cond_lora_B_w': _L0_cond_in['lora_B_w'], 'L1_cond_weights': _L1_cond_in['weights'], 'L2_cond_W': _L2_cond_in['W'], 'L2_cond_Wr': _L2_cond_in['Wr'], 'L2_cond_A': _L2_cond_in['A'], 'L2_cond_B': _L2_cond_in['B'], 'L3_cond_W': _L3_cond_in['W'], 'L3_cond_b': _L3_cond_in['b']}

def reference(x, itok_B_0_2, itok_B_0_15, itok_B_0_7, condB_coeff, mask_Bx4096x4096_ik1, L0_cond_W, L0_cond_lora_A, L0_cond_lora_B_w, L1_cond_weights, L2_cond_W, L2_cond_Wr, L2_cond_A, L2_cond_B, L3_cond_W, L3_cond_b):
    import jax
    import jax.numpy as jnp

    def _L0_cond_ref(x, labeler_index, W, lora_A, lora_B_w):
        import jax, jax.numpy as jnp
        import numpy as np
        B, S, D_IN, D_OUT = (4, 512, 1024, 1024)
        R, NUM_LABELERS = (32, 5)
        LORA_SCALING = 16 / 32
        base = jnp.einsum('bsi,oi->bso', x, W)
        labelers_A = lora_A[labeler_index]
        low = jnp.einsum('bsi,bir->bsr', x, labelers_A)
        delta = jnp.einsum('bsr,or->bso', low, lora_B_w) * LORA_SCALING
        return base + delta

    def _L1_cond_ref(x, weights, condition):
        import jax, jax.numpy as jnp
        import numpy as np
        NUM_CONDITIONS = 16
        IN_CH = 64
        OUT_CH = 64
        B = 64
        T = 1024
        W = weights[condition]
        return jnp.einsum('bct,bcd->bdt', x, W)

    def _L2_cond_ref(x, language_ids, W, Wr, A, B):
        import jax, jax.numpy as jnp
        import numpy as np
        TOP_K = 2
        LANG_BIAS = 5.0
        SCALING = 32.0 / 16.0
        LANGUAGE_PAD_ID = -1
        base = jnp.einsum('btd,od->bto', x, W)
        E = Wr.shape[0]
        logits = jnp.einsum('btd,ed->bte', x.astype(jnp.float32), Wr.astype(jnp.float32))
        expert_targets = language_ids
        valid = expert_targets >= 0
        tgt = jnp.where(valid, expert_targets, 0)
        bias = jax.nn.one_hot(tgt, E, dtype=logits.dtype) * LANG_BIAS
        bias = jnp.where(valid[:, None], bias, 0.0)
        logits = logits + bias[:, None, :]
        topw, topi = jax.lax.top_k(logits, TOP_K)
        weights = jax.nn.softmax(topw, axis=-1)
        gates = jnp.sum(jax.nn.one_hot(topi, E, dtype=weights.dtype) * weights[..., None], axis=-2)
        gates = gates.astype(x.dtype)
        h = jnp.einsum('btd,erd->bter', x, A)
        lora_out = jnp.einsum('bter,bte,eor->bto', h, gates, B)
        return base + SCALING * lora_out

    def _L3_cond_ref(hidden_states, W, b, coeff, mask):
        import jax, jax.numpy as jnp
        import numpy as np
        B, S, D_IN, D_OUT = (4, 128, 1024, 1024)
        output = jnp.einsum('bsi,oi->bso', hidden_states, W) + b
        sign = (2 * mask - 1).astype(hidden_states.dtype)
        diff = jnp.einsum('bsi,bio->bso', hidden_states, sign)
        return output + diff * coeff[:, None, None]
    x = x + _L0_cond_ref(x, itok_B_0_2, L0_cond_W, L0_cond_lora_A, L0_cond_lora_B_w)
    x = x + _L1_cond_ref(x, L1_cond_weights, itok_B_0_15)
    x = x + _L2_cond_ref(x, itok_B_0_7, L2_cond_W, L2_cond_Wr, L2_cond_A, L2_cond_B)
    x = x + _L3_cond_ref(x, L3_cond_W, L3_cond_b, condB_coeff, mask_Bx4096x4096_ik1)
    return x

_drawn_inputs = setup_inputs


def setup_inputs(seed=0):
    import zlib

    import numpy as np

    out = dict(_drawn_inputs(seed))
    spreads = {}
    factors = {'L3_cond_b': 8.0}
    for name, (base, spread) in spreads.items():
        noise = np.random.default_rng([zlib.crc32(name.encode()), seed]).standard_normal(out[name].shape)
        drawn = base * np.exp(spread * noise) if base else spread * noise
        out[name] = jnp.asarray(drawn.astype(out[name].dtype))
    for name, factor in factors.items():
        out[name] = (out[name] * factor).astype(out[name].dtype)
    return out
```

```python
from contextlib import ExitStack

import concourse.bass as bass
from concourse import mybir

F32 = mybir.dt.float32
F32R = mybir.dt.float32r
BF16 = mybir.dt.bfloat16
I32 = mybir.dt.int32
U32 = mybir.dt.uint32
ALU = mybir.AluOpType
ACT = mybir.ActivationFunctionType
AX = mybir.AxisListType

P = 128
SCRATCH = 1024


def layers_kernel(nc, x, cond, ids, coeff, mask, w0, bw, a_all, m2ext, b2, w3t, w1, bias, out):
    NB, TOK, D = x.shape
    PAIRS = NB // 2
    KT = D // P
    HALF = D // 2
    NEXT = m2ext.shape[1]
    E = 8
    R = (NEXT - D - E) // E
    ER = E * R
    RL = bw.shape[1]
    NL = a_all.shape[1] // RL
    NPV = NEXT + NL * RL
    V0 = D
    NV = NPV - D
    LOW0 = E + ER
    STEPS = 2 * KT
    RING = 8
    AHEAD = 4
    LANG_BIAS = 5.0
    cuts = [0, 388, 774, NEXT]
    assert NEXT == 1160 and NPV == 1320 and ER == P and STEPS == 16

    base = nc.sbuf_base + (-nc.sbuf_base) % 32
    place = [base]

    def at(name, shape, dt, offset=None):
        if offset is None:
            offset = place[0]
            size = 2 if dt == BF16 else 4
            for n in shape[1:]:
                size *= n
            place[0] += size + (-size) % 32
        return nc.alloc_sbuf_tensor_at(name, shape, dt, offset=offset), offset

    pv_hi, _ = at("pv_hi", [P, KT, NPV], F32R)
    pv_lo, o = at("pv_lo", [P, KT, NPV], F32R)
    pv_raw, _ = at("pv_raw", [P, KT, NPV], F32, o)
    bs, _ = at("bs", [P, NEXT], F32R)
    q_hi, o_m2 = at("q_hi", [P, KT, D], F32R)
    q_lo, o = at("q_lo", [P, KT, D], F32R)
    q_raw, _ = at("q_raw", [P, KT, D], F32, o)
    x3t, _ = at("x3t", [P, KT, 6, TOK], F32R)
    x3n, o_x3n = at("x3n", [P, HALF], F32)
    m2_hi, _ = at("m2_hi", [P, KT, NEXT], F32R, o_m2)
    m2_lo, o = at("m2_lo", [P, KT, NEXT], F32R, o_m2 + 4 * KT * NEXT)
    m2_raw, _ = at("m2_raw", [P, KT, NEXT], F32, o)
    assert o_m2 + 8 * KT * NEXT <= o_x3n + 2 * HALF
    b2_hi, _ = at("b2_hi", [P, D], F32R)
    b2_lo, o = at("b2_lo", [P, D], F32R)
    b2_raw, _ = at("b2_raw", [P, D], F32, o)
    x_in, _ = at("x_in", [P, D], F32)
    yt, o_yt = at("yt", [P, KT, 2, P], F32R)
    bw_raw, _ = at("bw_raw", [P, KT, RL], F32, o_yt)
    out_sb, _ = at("out_sb", [P, HALF], F32)
    sign, o_ring = at("sign", [P, RING, 2, HALF], F32R)
    mask_in, _ = at("mask_in", [P, RING, 2, HALF], I32, o_ring)
    m0_hi, m0_lo, m0_raw = [], [], []
    for b in range(2):
        o = o_ring + 4 * D * (4 + 2 * b)
        m0_hi.append(at(f"m0_hi{b}", [P, KT, P], F32R, o)[0])
        m0_lo.append(at(f"m0_lo{b}", [P, KT, P], F32R, o + 4 * D)[0])
        m0_raw.append(at(f"m0_raw{b}", [P, KT, P], F32, o + 4 * D)[0])
    ident, _ = at("ident", [P, P], F32)
    g, _ = at("g", [P, P], F32)
    low_all, o = at("low_all", [P, NL, RL], F32)
    low, _ = at("low", [P, 3, RL], F32)
    gated, _ = at("gated", [P, E, R], F32, o)
    gt_hi, _ = at("gt_hi", [P, P], F32R, o)
    gt_lo, _ = at("gt_lo", [P, P], F32R, o + 4 * P)
    low_t, _ = at("low_t", [P, P], F32R)
    cond_sb, _ = at("cond_sb", [1, NB], I32)
    ids_i, _ = at("ids_i", [P, 2, PAIRS], I32, o_x3n + 2 * HALF)
    ids_f, _ = at("ids_f", [P, 2, PAIRS], F32)
    coeff_sb, _ = at("coeff_sb", [P, PAIRS], F32)
    lab_hot, _ = at("lab_hot", [P, PAIRS, NL], BF16)
    lang_hot, _ = at("lang_hot", [P, PAIRS, E], BF16)
    iota, _ = at("iota", [P, E], F32)
    logits, _ = at("logits", [P, E], F32)
    top, _ = at("top", [P, E], F32)
    top_at, _ = at("top_at", [P, E], U32)
    top_f, _ = at("top_f", [P, 2], F32)
    ex, _ = at("ex", [P, 1], F32)
    den, _ = at("den", [P, 1], F32)
    rden, _ = at("rden", [P, 1], F32)
    w_a, _ = at("w_a", [P, 1], F32)
    w_b, _ = at("w_b", [P, 1], F32)
    gate_a, _ = at("gate_a", [P, E], F32)
    gate_b, _ = at("gate_b", [P, E], F32)
    gates, _ = at("gates", [P, E], F32)
    assert place[0] <= nc.sbuf_top, place[0]

    ctx = ExitStack()
    with ctx:
        def bank(name):
            return ctx.enter_context(nc.psum_tensor(name, [P, 512], F32))

        def sem(name):
            return ctx.enter_context(nc.semaphore(name))

        r0, r1, r2 = bank("r0"), bank("r1"), bank("r2")
        c_ps = [bank("c0"), bank("c1")]
        d_base, d_m0, d_m1 = bank("d_base"), bank("d_m0"), bank("d_m1")
        set_ps = [[r0, r1, r2], [c_ps[0], c_ps[1], d_base]]

        ident_ok = sem("ident_ok")
        tables_in = sem("tables_in")
        tables_ok = sem("tables_ok")
        m2_in = [sem(f"m2_in{k}") for k in range(KT)]
        m2_diag, m2_hi_ok, m2_lo_ok = sem("m2_diag"), sem("m2_hi_ok"), sem("m2_lo_ok")
        m0_in = [sem("m0_in0"), sem("m0_in1")]
        m0_diag, m0_hi_ok, m0_lo_ok, m0_used = sem("m0_diag"), sem("m0_hi_ok"), sem("m0_lo_ok"), sem("m0_used")
        bw_in = sem("bw_in")
        p_hi_ok, p_lo_ok = sem("p_hi_ok"), sem("p_lo_ok")
        av_in, av_hi_ok, av_lo_ok = sem("av_in"), sem("av_hi_ok"), sem("av_lo_ok")
        b2_in, b2_hi_ok, b2_lo_ok = sem("b2_in"), sem("b2_hi_ok"), sem("b2_lo_ok")
        q_in = [sem(f"q_in{k}") for k in range(KT)]
        q_diag, q_hi_ok, q_lo_ok = sem("q_diag"), sem("q_hi_ok"), sem("q_lo_ok")
        g_zero = sem("g_zero")
        x_ok, g_in, g_ok = sem("x_ok"), sem("g_in"), sem("g_ok")
        y_done, y_hi_ok, y_lo_ok = sem("y_done"), sem("y_hi_ok"), sem("y_lo_ok")
        v_done, low_step, low_ok = sem("v_done"), sem("low_step"), sem("low_ok")
        low_t_done, low_hi_ok, low_lo_ok = sem("low_t_done"), sem("low_hi_ok"), sem("low_lo_ok")
        lora_done, route, ex_ok, gated_ok = sem("lora_done"), sem("route"), sem("ex_ok"), sem("gated_ok")
        top_wait = sem("top_wait")
        gt_done, gt_hi_ok, gt_lo_ok = sem("gt_done"), sem("gt_hi_ok"), sem("gt_lo_ok")
        x3_done, x3n_ok = sem("x3_done"), sem("x3n_ok")
        x3t_done, x3t_hi_ok, x3t_lo_ok = sem("x3t_done"), sem("x3t_hi_ok"), sem("x3t_lo_ok")
        mask_ok = [sem(f"mask_ok{s}") for s in range(RING)]
        sign_even, sign_odd, slice_used = sem("sign_even"), sem("sign_odd"), sem("slice_used")
        bias_in, out_step, out_ok, stored = sem("bias_in"), sem("out_step"), sem("out_ok"), sem("stored")

        x_v = x.rearrange("(n b) c f -> n (b c) f", b=2)
        out_v = out.rearrange("(n b) c (h f) -> n h (b c) f", b=2, h=2)
        mask_v = mask.rearrange("(n b) (k p) (h f) -> n h k p b f", b=2, p=P, h=2)
        bias_v = bias.rearrange("(h a f) -> h a f", h=2, a=1)
        w0_v = w0.rearrange("(k p) (i c) -> i p k c", p=P, c=P)
        m2_v = m2ext.rearrange("(k p) n -> k p n", p=P)
        w3_v = w3t.rearrange("(k p) n -> k p n", p=P)
        bw_v = bw.rearrange("(k p) r -> p k r", p=P)
        a_v = a_all.rearrange("(k p) n -> p k n", p=P)

        def pair_of(view, t):
            return view[bass.ds(t, 1)]

        def y_half(yh):
            return yt[:, 4 * yh:4 * yh + 4]

        def in4(ps):
            return ps[:, :].rearrange("p (k n) -> p k n", k=4)

        block = ctx.enter_context(nc.Block())

        @block.sync
        def _(sp):
            def load_x(t):
                sp.dma_start(x_in[:, :], pair_of(x_v, t).rearrange("a p f -> p (a f)")).then_inc(x_ok, 16)

            def load_g(t):
                for b in range(2):
                    c = sp.value_load(cond_sb[0:1, bass.ds(2 * t + b, 1)], min_val=0, max_val=w1.shape[0] - 1)
                    sp.dma_start(g[TOK * b:TOK * b + TOK, TOK * b:TOK * b + TOK],
                                 w1[bass.ds(c, 1)].rearrange("a c d -> c (a d)")).then_inc(g_in, 16)

            def load_mask(q, s):
                sp.dma_start(mask_in[:, s % RING, :, :],
                             pair_of(mask_v[:, s // KT, s % KT], q).rearrange("a p b f -> p (a b) f"))\
                    .then_inc(mask_ok[s % RING], 16)

            def load_bias(half):
                sp.dma_start(out_sb[:, :], bias_v[half].to_broadcast([P, HALF])).then_inc(bias_in, 16)

            def store(q, half):
                sp.dma_start(pair_of(out_v[:, half], q).rearrange("a p f -> p (a f)"), out_sb[:, :])\
                    .then_inc(stored, 16)

            for i in range(2):
                sp.dma_start(m0_raw[i][:, :, :], w0_v[i]).then_inc(m0_in[i], 16)
            for k in range(KT):
                sp.dma_start(m2_raw[:, k, :], m2_v[k]).then_inc(m2_in[k], 16)
            sp.dma_start(bw_raw[:, :, :], bw_v).then_inc(bw_in, 16)
            sp.dma_start(pv_raw[:, :, NEXT:NPV], a_v).then_inc(av_in, 16)
            sp.dma_start(b2_raw[:, :], b2).then_inc(b2_in, 16)
            load_x(0)
            with sp.Fori(1, KT // 2) as i2:
                for j in range(2):
                    sp.wait_ge(m0_used, 2 * i2 + j - 1)
                    sp.dma_start(m0_raw[j][:, :, :],
                                 pair_of(w0_v, 2 * i2 + j).rearrange("a p k c -> p (a k) c")).then_inc(m0_in[j], 16)
            sp.wait_ge(tables_in, 48)
            sp.wait_ge(g_zero, 1)
            load_g(0)
            load_bias(0)
            for s in range(4):
                load_mask(0, s)
            sp.wait_ge(m0_used, KT + 1)
            for k in range(KT):
                sp.dma_start(q_raw[:, k, :], w3_v[k]).then_inc(q_in[k], 16)
            for s in range(4, RING):
                load_mask(0, s)
            sp.wait_ge(y_done, 2)
            load_x(1)
            sp.wait_ge(g_ok, 1)
            load_g(1)

            def iteration(t, prefetch, more):
                q = t - 1
                for s in range(STEPS):
                    if s == 3 and prefetch:
                        sp.wait_ge(y_done, 2 * t + 2)
                        load_x(t + 1)
                        sp.wait_ge(g_ok, t + 1)
                        load_g(t + 1)
                    if s < STEPS - RING or more:
                        sp.wait_ge(slice_used, STEPS * q + s + 1)
                        load_mask(q if s < STEPS - RING else q + 1, (s + RING) % STEPS)
                    if s == 9:
                        sp.wait_ge(out_ok, 2 * q + 2)
                        store(q, 0)
                    if s == 11:
                        sp.wait_ge(stored, 16 * (2 * q + 1))
                        load_bias(1)
                sp.wait_ge(out_ok, 2 * q + 3)
                store(q, 1)
                if more:
                    sp.wait_ge(stored, 16 * (2 * q + 2))
                    load_bias(0)

            with sp.Fori(1, PAIRS - 1) as t:
                iteration(t, True, True)
            iteration(PAIRS - 1, False, True)
            iteration(PAIRS, False, False)
            sp.wait_ge(stored, 16 * 2 * PAIRS)

        @block.gpsimd
        def _(pool):
            nc.gpsimd.memset(ident[:, :], 0.0).then_inc(ident_ok, 1)
            nc.gpsimd.memset(g[:, :], 0.0).then_inc(g_zero, 1)
            pool.wait_ge(ident_ok, 1)
            nc.gpsimd.affine_select(out=ident[:, :], in_=ident[:, :], compare_op=ALU.not_equal, fill=1.0,
                                    base=0, pattern=[[-1, P]], channel_multiplier=1).then_inc(ident_ok, 1)

        @block.scalar
        def _(act):
            def hi(dst, src, scale=1.0):
                return nc.scalar.activation(dst, src, ACT.Copy, scale=scale)

            act.dma_start(ids_i[:, :, :], ids).then_inc(tables_in, 16)
            act.dma_start(coeff_sb[:, :], coeff).then_inc(tables_in, 16)
            act.dma_start(cond_sb[:, :], cond.rearrange("(a n) -> a n", a=1)).then_inc(tables_in, 16)
            for i in range(2):
                act.wait_ge(m0_diag, i + 1)
                hi(m0_hi[i][:, :, :], m0_raw[i][:, :, :]).then_inc(m0_hi_ok, 1)
            for k in range(KT):
                act.wait_ge(m2_diag, k + 1)
                hi(m2_hi[:, k, :], m2_raw[:, k, :]).then_inc(m2_hi_ok, 1)
            act.wait_ge(av_in, 16)
            hi(pv_hi[:, :, NEXT:NPV], pv_raw[:, :, NEXT:NPV]).then_inc(av_hi_ok, 1)
            act.wait_ge(b2_in, 16)
            hi(b2_hi[:, :], b2_raw[:, :]).then_inc(b2_hi_ok, 1)

            def p_hi(i, j):
                act.wait_ge(m0_used, i + 1)
                for c in range(3):
                    w = cuts[c + 1] - cuts[c]
                    dst = pv_hi[:, bass.ds(i, 1), cuts[c]:cuts[c + 1]].rearrange("p a n -> p (a n)")
                    hi(dst, set_ps[j][c][:, 0:w]).then_inc(p_hi_ok, 1)

            with act.Fori(0, KT // 2 - 1) as i2:
                for j in range(2):
                    p_hi(2 * i2 + j, j)
                    act.wait_ge(m0_diag, 2 * i2 + j + 3)
                    hi(m0_hi[j][:, :, :], m0_raw[j][:, :, :]).then_inc(m0_hi_ok, 1)
            p_hi(KT - 2, 0)
            act.wait_ge(bw_in, 16)
            for c in range(3):
                ins = hi(m0_hi[0][:, :, RL * c:RL * c + RL], bw_raw[:, :, :], scale=0.5)
            ins.then_inc(m0_hi_ok, 1)
            p_hi(KT - 1, 1)
            act.wait_ge(m0_used, KT + 1)
            for c in range(3):
                w = cuts[c + 1] - cuts[c]
                hi(bs[0:3 * RL, cuts[c]:cuts[c + 1]], set_ps[0][c][0:3 * RL, 0:w]).then_inc(p_hi_ok, 1)

            def to_sign(q, s):
                act.wait_ge(mask_ok[s % RING], 16 * (2 * q + s // RING + 1))
                nc.scalar.activation(sign[:, s % RING, :, :], mask_in[:, s % RING, :, :], ACT.Copy,
                                     scale=2.0, bias=-1.0).then_inc(sign_odd, 1)

            def y_hi(t, yh, ps):
                act.wait_ge(y_done, 2 * t + yh + 1)
                hi(y_half(yh)[:, :, 0, :], in4(ps)).then_inc(y_hi_ok, 1)

            def x3t_hi(t, h):
                act.wait_ge(x3t_done, 2 * t + h + 1)
                hi(x3t[:, 4 * h:4 * h + 4, 1:3, :],
                   r1[:, :].rearrange("p (k b n) -> p k b n", k=4, b=2)).then_inc(x3t_hi_ok, 1)

            def x3_out(t, h):
                act.wait_ge(x3_done, 2 * t + h + 1)
                if h == 1:
                    act.wait_ge(x3t_done, 2 * t + 1)
                nc.scalar.activation(x3n[:, :], c_ps[h][:, :], ACT.Copy).then_inc(x3n_ok, 1)

            def iteration(t, front, back, more):
                q = t - 1
                if front:
                    y_hi(t, 0, r0)
                if back:
                    x3t_hi(q, 1)
                if front:
                    y_hi(t, 1, r2)
                for s in range(STEPS):
                    if back and s % 2 == 1 and (s + AHEAD < STEPS or more):
                        to_sign(q if s + AHEAD < STEPS else q + 1, (s + AHEAD) % STEPS)
                    if not back and s % 2 == 1:
                        k = s // 2
                        act.wait_ge(q_diag, k + 1)
                        hi(q_hi[:, k, :], q_raw[:, k, :]).then_inc(q_hi_ok, 1)
                    if front and s == 6:
                        act.wait_ge(low_t_done, t + 1)
                        hi(low_t[0:3 * RL, :], r1[0:3 * RL, 0:P]).then_inc(low_hi_ok, 1)
                    if front and s == 9:
                        act.wait_ge(route, 11 * t + 2)
                        nc.scalar.activation(ex[:, :], top[:, 0:1], ACT.Exp, scale=-1.0, bias=top[:, 1:2])\
                            .then_inc(ex_ok, 1)
                    if front and s == 12:
                        act.wait_ge(gt_done, t + 1)
                        hi(gt_hi[:, :], r2[:, 0:P]).then_inc(gt_hi_ok, 1)
                    if front and s == 13:
                        x3_out(t, 0)
                    if front and s == 15:
                        x3t_hi(t, 0)
                if front:
                    x3_out(t, 1)
                if not back:
                    for s in range(1, AHEAD, 2):
                        to_sign(0, s)

            iteration(0, True, False, True)
            with act.Fori(1, PAIRS - 1) as t:
                iteration(t, True, True, True)
            iteration(PAIRS - 1, True, True, True)
            iteration(PAIRS, False, True, False)

        @block.vector
        def _(dve):
            def lo(dst, src, hi_part):
                return nc.vector.tensor_tensor(dst, src, hi_part.bitcast(F32), ALU.subtract)

            def add_diag(tile):
                return nc.vector.tensor_tensor(tile, tile, ident[:, :], ALU.add)

            dve.sem_inc(out_ok, 1)
            dve.wait_ge(ident_ok, 2)
            for i in range(2):
                dve.wait_ge(m0_in[i], 16)
                add_diag(m0_raw[i][:, i, :]).then_inc(m0_diag, 1)
            for i in range(2):
                dve.wait_ge(m0_hi_ok, i + 1)
                lo(m0_lo[i][:, :, :], m0_raw[i][:, :, :], m0_hi[i][:, :, :]).then_inc(m0_lo_ok, 1)

            def m2_diagonal(k):
                dve.wait_ge(m2_in[k], 16)
                add_diag(m2_raw[:, k, P * k:P * k + P]).then_inc(m2_diag, 1)

            m2_diagonal(0)
            for k in range(KT):
                if k + 1 < KT:
                    m2_diagonal(k + 1)
                dve.wait_ge(m2_hi_ok, k + 1)
                lo(m2_lo[:, k, :], m2_raw[:, k, :], m2_hi[:, k, :]).then_inc(m2_lo_ok, 1)
            dve.wait_ge(av_hi_ok, 1)
            lo(pv_lo[:, :, NEXT:NPV], pv_raw[:, :, NEXT:NPV], pv_hi[:, :, NEXT:NPV]).then_inc(av_lo_ok, 1)
            dve.wait_ge(b2_hi_ok, 1)
            lo(b2_lo[:, :], b2_raw[:, :], b2_hi[:, :]).then_inc(b2_lo_ok, 1)

            dve.wait_ge(tables_in, 48)
            nc.vector.tensor_copy(ids_f[:, :, :], ids_i[:, :, :]).then_inc(tables_ok, 1)
            for e in range(E):
                nc.vector.memset(iota[:, e:e + 1], float(e)).then_inc(tables_ok, 1)
            dve.wait_ge(tables_ok, 1)
            for e in range(NL):
                nc.vector.tensor_scalar(lab_hot[:, :, e], ids_f[:, 0, :], float(e), None, ALU.is_equal)\
                    .then_inc(tables_ok, 1)
            for e in range(E):
                nc.vector.tensor_scalar(lang_hot[:, :, e], ids_f[:, 1, :], float(e), LANG_BIAS,
                                        ALU.is_equal, ALU.mult).then_inc(tables_ok, 1)
            TABLES = 1 + E + NL + E

            def p_lo(i, j):
                for c in range(3):
                    w = cuts[c + 1] - cuts[c]
                    dve.wait_ge(p_hi_ok, 3 * i + c + 1)
                    at_lo = pv_lo[:, bass.ds(i, 1), cuts[c]:cuts[c + 1]].rearrange("p a n -> p (a n)")
                    at_hi = pv_hi[:, bass.ds(i, 1), cuts[c]:cuts[c + 1]].rearrange("p a n -> p (a n)")
                    lo(at_lo, set_ps[j][c][:, 0:w], at_hi).then_inc(p_lo_ok, 1)

            with dve.Fori(0, KT // 2 - 1) as i2:
                for j in range(2):
                    dve.wait_ge(m0_in[j], 16 * (i2 + 2))
                    add_diag(m0_raw[j][:, bass.ds(2 * i2 + j + 2, 1), :].rearrange("p a n -> p (a n)"))\
                        .then_inc(m0_diag, 1)
                    p_lo(2 * i2 + j, j)
                    dve.wait_ge(m0_hi_ok, 2 * i2 + j + 3)
                    lo(m0_lo[j][:, :, :], m0_raw[j][:, :, :], m0_hi[j][:, :, :]).then_inc(m0_lo_ok, 1)
            p_lo(KT - 2, 0)
            dve.wait_ge(m0_hi_ok, KT + 1)
            dve.wait_ge(m0_used, KT - 1)
            for c in range(3):
                cols = slice(RL * c, RL * c + RL)
                ins = nc.vector.scalar_tensor_tensor(out=m0_lo[0][:, :, cols], in0=bw_raw[:, :, :], scalar=0.5,
                                                     in1=m0_hi[0][:, :, cols].bitcast(F32),
                                                     op0=ALU.mult, op1=ALU.subtract)
            ins.then_inc(m0_lo_ok, 1)
            p_lo(KT - 1, 1)
            for c in range(3):
                w = cuts[c + 1] - cuts[c]
                dve.wait_ge(p_hi_ok, 3 * KT + c + 1)
                rows = bs[RL:2 * RL, cuts[c]:cuts[c + 1]]
                lo(rows, set_ps[0][c][RL:2 * RL, 0:w], rows).then_inc(p_lo_ok, 1)

            def make_g(t):
                dve.wait_ge(g_in, 32 * (t + 1))
                add_diag(g[:, :]).then_inc(g_ok, 1)

            def to_sign(q, s):
                dve.wait_ge(mask_ok[s % RING], 16 * (2 * q + s // RING + 1))
                nc.vector.tensor_scalar(sign[:, s % RING, :, :], mask_in[:, s % RING, :, :], 2.0, -1.0,
                                        ALU.mult, ALU.add).then_inc(sign_even, 1)

            def y_lo(t, yh, ps):
                dve.wait_ge(y_hi_ok, 2 * t + yh + 1)
                lo(y_half(yh)[:, :, 1, :], in4(ps), y_half(yh)[:, :, 0, :]).then_inc(y_lo_ok, 1)

            def x3t_lo(t, h):
                dve.wait_ge(x3t_hi_ok, 2 * t + h + 1)
                tiles = slice(4 * h, 4 * h + 4)
                ps = r1[:, :].rearrange("p (k b n) -> p k b n", k=4, b=2)
                lo(x3t[:, tiles, 0:4:3, :], ps, x3t[:, tiles, 1:3, :])
                lo(x3t[:, tiles, 4:6, :], ps, x3t[:, tiles, 1:3, :]).then_inc(x3t_lo_ok, 1)

            def pick_low(t):
                dve.wait_ge(v_done, t + 1)
                hot = lab_hot[:, bass.ds(t, 1), :].rearrange("p a l -> p (a l)").unsqueeze(2)
                nc.vector.tensor_tensor(
                    low_all[:, :, :], r0[:, LOW0:NV].rearrange("p (l r) -> p l r", l=NL),
                    hot.to_broadcast([P, NL, RL]), ALU.mult).then_inc(low_step, 1)
                dve.wait_ge(low_step, 2 * t + 1)
                nc.vector.tensor_reduce(low[:, 0, :], low_all[:, :, :].rearrange("p l r -> p r l"), AX.X, ALU.add)\
                    .then_inc(low_step, 1)
                dve.wait_ge(low_step, 2 * t + 2)
                nc.vector.tensor_copy(low[:, 1:3, :], low[:, 0:1, :].to_broadcast([P, 2, RL])).then_inc(low_ok, 1)

            def route_top(t):
                dve.wait_ge(lora_done, t + 1)
                nc.vector.tensor_tensor(logits[:, :], r0[:, 0:E],
                                        lang_hot[:, bass.ds(t, 1), :].rearrange("p a e -> p (a e)"), ALU.add)\
                    .then_inc(route, 1)
                dve.wait_ge(route, 11 * t + 1).then_inc(top_wait, 1)
                nc.vector.max(top[:, :], logits[:, :]).then_inc(route, 1)
                dve.wait_ge(route, 11 * t + 2).then_inc(top_wait, 1)
                nc.vector.max_index(top_at[:, :], top[:, :], logits[:, :]).then_inc(route, 1)
                dve.wait_ge(route, 11 * t + 3)
                nc.vector.tensor_copy(top_f[:, :], top_at[:, 0:2]).then_inc(route, 1)

            def route_gates(t):
                dve.wait_ge(ex_ok, t + 1)
                nc.vector.tensor_scalar(den[:, :], ex[:, :], 1.0, None, ALU.add).then_inc(route, 1)
                dve.wait_ge(route, 11 * t + 5)
                nc.vector.reciprocal(rden[:, :], den[:, :]).then_inc(route, 1)
                dve.wait_ge(route, 11 * t + 6)
                nc.vector.tensor_scalar(w_a[:, :], rden[:, :], 2.0, None, ALU.mult).then_inc(route, 1)
                nc.vector.tensor_scalar(w_b[:, :], rden[:, :], ex[:, 0:1], 2.0, ALU.mult, ALU.mult)\
                    .then_inc(route, 1)
                dve.wait_ge(route, 11 * t + 8)
                nc.vector.tensor_scalar(gate_a[:, :], iota[:, :], top_f[:, 0:1], w_a[:, 0:1],
                                        ALU.is_equal, ALU.mult).then_inc(route, 1)
                nc.vector.tensor_scalar(gate_b[:, :], iota[:, :], top_f[:, 1:2], w_b[:, 0:1],
                                        ALU.is_equal, ALU.mult).then_inc(route, 1)
                dve.wait_ge(route, 11 * t + 10)
                nc.vector.tensor_tensor(gates[:, :], gate_a[:, :], gate_b[:, :], ALU.add).then_inc(route, 1)
                dve.wait_ge(route, 11 * t + 11)
                nc.vector.tensor_tensor(gated[:, :, :], r0[:, E:LOW0].rearrange("p (e r) -> p e r", e=E),
                                        gates[:, :].unsqueeze(2).to_broadcast([P, E, R]), ALU.mult)\
                    .then_inc(gated_ok, 1)

            def finish_half(q, h):
                n = 4 * (2 * q + h)
                dve.wait_ge(slice_used, STEPS * q + KT * (h + 1))
                dve.wait_ge(bias_in, 16 * (2 * q + h + 1))
                nc.vector.tensor_tensor(out_sb[:, :], d_base[:, :], out_sb[:, :], ALU.add).then_inc(out_step, 1)
                for part in range(2):
                    for b, ps in enumerate((d_m0, d_m1)):
                        mine = slice(TOK * b, TOK * b + TOK)
                        if b == 0:
                            dve.wait_ge(out_step, n + (1 if part == 0 else 2))
                        elif part == 1:
                            dve.wait_ge(out_step, n + 3)
                        ins = nc.vector.scalar_tensor_tensor(
                            out=out_sb[mine, :], in0=ps[TOK * part:TOK * part + TOK, :],
                            scalar=coeff_sb[mine, bass.ds(q, 1)], in1=out_sb[mine, :],
                            op0=ALU.mult, op1=ALU.add)
                        if part == 1 and b == 1:
                            ins.then_inc(out_ok, 1)
                        else:
                            ins.then_inc(out_step, 1)

            def iteration(t, front, back, prefetch, more):
                q = t - 1
                if front:
                    y_lo(t, 0, r0)
                if back:
                    x3t_lo(q, 1)
                if front:
                    y_lo(t, 1, r2)
                for s in range(STEPS):
                    if back and s % 2 == 0 and (s + AHEAD < STEPS or more):
                        to_sign(q if s + AHEAD < STEPS else q + 1, (s + AHEAD) % STEPS)
                    if not back and s % 2 == 0:
                        k = s // 2
                        dve.wait_ge(q_in[k], 16)
                        add_diag(q_raw[:, k, P * k:P * k + P]).then_inc(q_diag, 1)
                    if not back and s % 2 == 1:
                        k = s // 2
                        dve.wait_ge(q_hi_ok, k + 1)
                        lo(q_lo[:, k, :], q_raw[:, k, :], q_hi[:, k, :]).then_inc(q_lo_ok, 1)
                    if front and s == 4:
                        pick_low(t)
                    if front and s == 6:
                        dve.wait_ge(low_hi_ok, t + 1)
                        rows = low_t[2 * RL:3 * RL, :]
                        lo(rows, r1[2 * RL:3 * RL, 0:P], rows).then_inc(low_lo_ok, 1)
                    if back and s == 7:
                        finish_half(q, 0)
                    if front and s == 8:
                        route_top(t)
                    if front and s == 9:
                        route_gates(t)
                    if front and s == 12:
                        dve.wait_ge(gt_hi_ok, t + 1)
                        lo(gt_lo[:, :], r2[:, 0:P], gt_hi[:, :]).then_inc(gt_lo_ok, 1)
                    if prefetch and s == 13:
                        make_g(t + 1)
                    if front and s == 15:
                        x3t_lo(t, 0)
                if not back:
                    for s in range(0, AHEAD, 2):
                        to_sign(0, s)
                if back:
                    finish_half(q, 1)

            dve.wait_ge(tables_ok, TABLES)
            make_g(0)
            iteration(0, True, False, True, True)
            with dve.Fori(1, PAIRS - 1) as t:
                iteration(t, True, True, True, True)
            iteration(PAIRS - 1, True, True, False, True)
            iteration(PAIRS, False, True, False, False)

        @block.tensor
        def _(pe):
            mm = nc.tensor.matmul

            def setup_tile(j, first, width):
                hi_t, lo_t = m0_hi[j], m0_lo[j]
                for k in range(KT):
                    if first:
                        pe.wait_ge(m2_lo_ok, k + 1)
                    for n, (a, b) in enumerate(((hi_t, m2_hi), (hi_t, m2_lo), (lo_t, m2_hi))):
                        for c in range(3):
                            w = cuts[c + 1] - cuts[c]
                            ins = mm(set_ps[j][c][0:width, 0:w], a[:, k, 0:width], b[:, k, cuts[c]:cuts[c + 1]],
                                     start=(k == 0 and n == 0), stop=(k == KT - 1 and n == 2))
                ins.then_inc(m0_used, 1)

            for j in range(2):
                pe.wait_ge(m0_lo_ok, j + 1)
                setup_tile(j, j == 0, P)
            with pe.Fori(1, KT // 2) as i2:
                for j in range(2):
                    pe.wait_ge(m0_lo_ok, 2 * i2 + j + 1)
                    pe.wait_ge(p_lo_ok, 3 * (2 * i2 + j - 1))
                    setup_tile(j, False, P)
            pe.wait_ge(m0_lo_ok, KT + 1)
            pe.wait_ge(p_lo_ok, 3 * (KT - 1))
            setup_tile(0, False, 3 * RL)

            def y_part(t, yh, ps):
                if yh == 0:
                    pe.wait_ge(x_ok, 16 * (t + 1))
                    pe.wait_ge(g_ok, t + 1)
                for k in range(4):
                    n = P * (4 * yh + k)
                    ins = mm(ps[:, P * k:P * k + P], x_in[:, n:n + P], g[:, :], start=True, stop=True)
                ins.then_inc(y_done, 1)

            def v_step(t, k):
                if k % 4 == 0:
                    pe.wait_ge(y_lo_ok, 2 * t + k // 4 + 1)
                for n, (a, b) in enumerate(((0, pv_hi), (0, pv_lo), (1, pv_hi))):
                    ins = mm(r0[:, 0:NV], yt[:, k, a, :], b[:, k, V0:NPV],
                             start=(k == 0 and n == 0), stop=(k == KT - 1 and n == 2), skip_group_check=True)
                if k == KT - 1:
                    ins.then_inc(v_done, 1)

            def low_turn(t):
                pe.wait_ge(low_ok, t + 1)
                if isinstance(t, int) and t == 0:
                    pe.wait_ge(p_lo_ok, 3 * (KT + 1))
                else:
                    pe.wait_ge(x3t_lo_ok, 2 * t)
                nc.tensor.transpose(r1[0:3 * RL, 0:P], low[:, :, :].rearrange("p c r -> p (c r)"), ident[:, :])\
                    .then_inc(low_t_done, 1)

            def lora(t):
                pe.wait_ge(low_lo_ok, t + 1)
                mm(r0[:, 0:LOW0], low_t[0:3 * RL, :], bs[0:3 * RL, D:NEXT], start=False, stop=True,
                   skip_group_check=True).then_inc(lora_done, 1)

            def x3_step(t, h, k):
                cols = slice(HALF * h, HALF * h + HALF)
                for n, (a, b) in enumerate(((0, pv_hi), (0, pv_lo), (1, pv_hi))):
                    mm(c_ps[h][:, :], yt[:, k, a, :], b[:, k, cols], start=(k == 0 and n == 0), stop=False)

            def x3_tail(t, h):
                cols = slice(HALF * h, HALF * h + HALF)
                pe.wait_ge(gt_lo_ok, t + 1)
                mm(c_ps[h][:, :], low_t[0:3 * RL, :], bs[0:3 * RL, cols], start=False, stop=False)
                mm(c_ps[h][:, :], gt_hi[:, :], b2_hi[:, cols], start=False, stop=False)
                mm(c_ps[h][:, :], gt_hi[:, :], b2_lo[:, cols], start=False, stop=False)
                mm(c_ps[h][:, :], gt_lo[:, :], b2_hi[:, cols], start=False, stop=True).then_inc(x3_done, 1)

            def turn_gated(t):
                pe.wait_ge(gated_ok, t + 1)
                nc.tensor.transpose(r2[:, 0:P], gated[:, :, :].rearrange("p e r -> p (e r)"), ident[:, :])\
                    .then_inc(gt_done, 1)

            def turn_x3(t, h):
                pe.wait_ge(x3n_ok, 2 * t + h + 1)
                if h == 1:
                    pe.wait_ge(x3t_lo_ok, 2 * t + 1)
                for k in range(4):
                    ins = nc.tensor.transpose(r1[:, P * k:P * k + P], x3n[:, P * k:P * k + P], ident[:, :])
                ins.then_inc(x3t_done, 1)

            def back_step(q, s):
                h, k = s // KT, s % KT
                cols = slice(HALF * h, HALF * h + HALF)
                if k == 0:
                    pe.wait_ge(out_ok, 2 * q + h + 1)
                if s == 0 or s == 4:
                    pe.wait_ge(x3t_lo_ok, 2 * q + s // 4 + 1)
                pe.wait_ge(sign_even if s % 2 == 0 else sign_odd, STEPS // 2 * q + s // 2 + 1)
                for b, ps in enumerate((d_m0, d_m1)):
                    mm(ps[:, :], x3t[:, k, 2 * b:2 * b + 2, :].rearrange("p l n -> p (l n)"), sign[:, s % RING, b, :],
                       start=(k == 0), stop=(k == KT - 1))
                ins = None
                for n, (a, b) in enumerate(((1, q_hi), (1, q_lo), (4, q_hi))):
                    ins = mm(d_base[:, :], x3t[:, k, a:a + 2, :].rearrange("p b n -> p (b n)"), b[:, k, cols],
                             start=(k == 0 and n == 0), stop=(k == KT - 1 and n == 2))
                ins.then_inc(slice_used, 1)

            fill = [
                [("v", 2), ("v", 3)], [("v", 4), ("v", 5)], [("v", 6), ("v", 7)], [("x3", 0, 0)],
                [("x3", 0, 1)], [("low",), ("x3", 0, 2)], [("x3", 0, 3)],
                [("lora",), ("x3", 0, 4), ("x3", 0, 5), ("x3", 0, 6), ("x3", 0, 7), ("x3", 1, 0)],
                [("x3", 1, 1)], [("x3", 1, 2)], [("x3", 1, 3)], [("gated",), ("x3", 1, 4)],
                [("tail", 0)], [("x3", 1, 5)], [("turn", 0)], [("x3", 1, 6), ("x3", 1, 7), ("tail", 1)],
            ]

            def front_work(t, item):
                kind = item[0]
                if kind == "v":
                    v_step(t, item[1])
                elif kind == "low":
                    low_turn(t)
                elif kind == "lora":
                    lora(t)
                elif kind == "x3":
                    x3_step(t, item[1], item[2])
                elif kind == "gated":
                    turn_gated(t)
                elif kind == "tail":
                    x3_tail(t, item[1])
                else:
                    turn_x3(t, item[1])

            def iteration(t, front, back):
                q = t - 1
                if front:
                    y_part(t, 0, r0)
                if back:
                    turn_x3(q, 1)
                if front:
                    y_part(t, 1, r2)
                    v_step(t, 0)
                    v_step(t, 1)
                for s in range(STEPS):
                    if back:
                        back_step(q, s)
                    if front:
                        for item in fill[s]:
                            front_work(t, item)

            pe.wait_ge(ident_ok, 2)
            pe.wait_ge(av_lo_ok, 1)
            pe.wait_ge(b2_lo_ok, 1)
            pe.wait_ge(p_lo_ok, 3 * (KT + 1))
            iteration(0, True, False)
            pe.wait_ge(q_lo_ok, KT)
            with pe.Fori(1, PAIRS) as t:
                iteration(t, True, True)
            iteration(PAIRS, False, True)


def kernel(**inputs):
    import numpy as np
    import concourse.bacc as bacc
    from concourse.bass_utils import run_bass_kernel_spmd

    def arr(name):
        return np.asarray(inputs[name])

    x = arr("x")
    pairs = x.shape[0] // 2

    def per_token(a):
        return np.repeat(a.reshape(pairs, 2).T, 64, axis=0)

    expert_a = arr("L2_cond_A")
    expert_b = arr("L2_cond_B")
    labeler_a = arr("L0_cond_lora_A")
    d = x.shape[2]
    arrays = {
        "x": x,
        "cond": arr("itok_B_0_15"),
        "ids": np.stack([per_token(arr("itok_B_0_2")), per_token(arr("itok_B_0_7"))], axis=1),
        "coeff": per_token(arr("condB_coeff")),
        "mask": arr("mask_Bx4096x4096_ik1"),
        "w0": arr("L0_cond_W"),
        "bw": arr("L0_cond_lora_B_w"),
        "a_all": labeler_a.transpose(1, 0, 2).reshape(d, -1),
        "m2ext": np.concatenate([arr("L2_cond_W").T, arr("L2_cond_Wr").T, expert_a.reshape(-1, d).T], axis=1),
        "b2": expert_b.transpose(0, 2, 1).reshape(-1, d),
        "w3t": arr("L3_cond_W").T,
        "w1": arr("L1_cond_weights"),
        "bias": arr("L3_cond_b"),
    }
    nc = bacc.Bacc("TRN2", target_bir_lowering=False, num_devices=1, dynamic_dma_scratch_size=SCRATCH)
    feed, args = {}, {}
    for name, a in arrays.items():
        a = np.ascontiguousarray(a)
        feed[f"in_{name}"] = a
        args[name] = nc.dram_tensor(f"in_{name}", a.shape, mybir.dt.from_np(a.dtype), kind="ExternalInput").ap()
    args["out"] = nc.dram_tensor("out_x", x.shape, F32, kind="ExternalOutput").ap()
    layers_kernel(nc, **args)
    result = run_bass_kernel_spmd(nc, [feed], core_ids=[0])
    return result.results[0]["out_x"]
```

```python
from contextlib import ExitStack

import concourse.bass as bass
from concourse import mybir

F32 = mybir.dt.float32
F32R = mybir.dt.float32r
BF16 = mybir.dt.bfloat16
I32 = mybir.dt.int32
U32 = mybir.dt.uint32
ALU = mybir.AluOpType
ACT = mybir.ActivationFunctionType
AX = mybir.AxisListType

P = 128
SCRATCH = 1024


def layers_kernel(nc, x, picks, lang, coeff, mask, w0, bw, labelers, m2ext, b2, w3t, w1, bias, out):
    NB, TOK, D = x.shape
    PAIRS = NB // 2
    KT = D // P
    HALF = D // 2
    NEXT = m2ext.shape[1]
    E = 8
    R = (NEXT - D - E) // E
    ER = E * R
    RL = bw.shape[1]
    NPV = NEXT + 2 * RL
    NV = 256
    V0 = NPV - NV
    PX = D - V0
    A0 = PX + E
    LOW0 = A0 + ER
    STEPS = 2 * KT
    RING = 8
    AHEAD = 4
    LANG_BIAS = 5.0
    cuts = [0, 388, 774, NEXT]
    assert NEXT == 1160 and NPV == 1224 and ER == P and 4 * RL == P and STEPS == 16

    base = nc.sbuf_base + (-nc.sbuf_base) % 32
    place = [base]

    def at(name, shape, dt, offset=None):
        if offset is None:
            offset = place[0]
            size = 2 if dt == BF16 else 4
            for n in shape[1:]:
                size *= n
            place[0] += size + (-size) % 32
        return nc.alloc_sbuf_tensor_at(name, shape, dt, offset=offset), offset

    pv_hi, _ = at("pv_hi", [P, KT, NPV], F32R)
    pv_lo, _ = at("pv_lo", [P, KT, NPV], F32R)
    bs, _ = at("bs", [P, NEXT], F32R)
    q_lo, o_m2 = at("q_lo", [P, KT, D], F32R)
    q_raw, _ = at("q_raw", [P, KT, D], F32, o_m2)
    x3n, _ = at("x3n", [P, HALF], F32)
    gated, _ = at("gated", [P, E, R], F32)
    low, _ = at("low", [P, 4, RL], F32)
    gt_hi, _ = at("gt_hi", [P, P], F32R)
    gt_lo, _ = at("gt_lo", [P, P], F32R)
    o_m2_lo = o_m2 + 4 * KT * NEXT
    assert place[0] <= o_m2_lo
    place[0] = o_m2_lo
    q_hi, _ = at("q_hi", [P, KT, D], F32R)
    x3t, _ = at("x3t", [P, KT, 6, TOK], F32R)
    m2_hi, _ = at("m2_hi", [P, KT, NEXT], F32R, o_m2)
    m2_lo, o = at("m2_lo", [P, KT, NEXT], F32R, o_m2_lo)
    m2_raw, _ = at("m2_raw", [P, KT, NEXT], F32, o)
    assert o_m2_lo + 4 * KT * NEXT <= place[0]
    b2_hi, _ = at("b2_hi", [P, D], F32R)
    b2_lo, o = at("b2_lo", [P, D], F32R)
    b2_raw, _ = at("b2_raw", [P, D], F32, o)
    x_in, o = at("x_in", [P, D], F32)
    last_out = [at(f"last_out{h}", [P, HALF], F32, o + 4 * HALF * h)[0] for h in range(2)]
    yt, o_yt = at("yt", [P, KT, 2, P], F32R)
    bw_raw, _ = at("bw_raw", [P, KT, RL], F32, o_yt)
    out_sb, _ = at("out_sb", [P, HALF], F32)
    sign, o_ring = at("sign", [P, RING, 2, HALF], F32R)
    mask_in, _ = at("mask_in", [P, RING, 2, HALF], I32, o_ring)
    m0_hi, m0_lo, m0_raw = [], [], []
    for b in range(2):
        o = o_ring + 4 * D * (4 + 2 * b)
        m0_hi.append(at(f"m0_hi{b}", [P, KT, P], F32R, o)[0])
        m0_lo.append(at(f"m0_lo{b}", [P, KT, P], F32R, o + 4 * D)[0])
        m0_raw.append(at(f"m0_raw{b}", [P, KT, P], F32, o + 4 * D)[0])
    ident, _ = at("ident", [P, P], F32)
    g, _ = at("g", [P, P], F32)
    a_raw, _ = at("a_raw", [P, 2, KT, RL], F32)
    low_t, _ = at("low_t", [P, P], F32R)
    picks_sb, _ = at("picks_sb", [1, 2, NB], I32)
    lang_i, _ = at("lang_i", [P, PAIRS], I32)
    lang_f, _ = at("lang_f", [P, PAIRS], F32)
    coeff_sb, _ = at("coeff_sb", [P, PAIRS], F32)
    lang_hot, _ = at("lang_hot", [P, PAIRS, E], BF16)
    iota, _ = at("iota", [P, E], F32)
    logits, _ = at("logits", [P, E], F32)
    top, _ = at("top", [P, E], F32)
    top_at, _ = at("top_at", [P, E], U32)
    top_f, _ = at("top_f", [P, 2], F32)
    ex, _ = at("ex", [P, 1], F32)
    den, _ = at("den", [P, 1], F32)
    rden, _ = at("rden", [P, 1], F32)
    w_a, _ = at("w_a", [P, 1], F32)
    w_b, _ = at("w_b", [P, 1], F32)
    gate_a, _ = at("gate_a", [P, E], F32)
    gate_b, _ = at("gate_b", [P, E], F32)
    gates, _ = at("gates", [P, E], F32)
    assert place[0] <= nc.sbuf_top, place[0]

    ctx = ExitStack()
    with ctx:
        def bank(name):
            return ctx.enter_context(nc.psum_tensor(name, [P, 512], F32))

        def sem(name):
            return ctx.enter_context(nc.semaphore(name))

        r0, r1, r2 = bank("r0"), bank("r1"), bank("r2")
        c_ps = [bank("c0"), bank("c1")]
        d_base, d_m0, d_m1 = bank("d_base"), bank("d_m0"), bank("d_m1")
        set_ps = [[c_ps[0], c_ps[1], d_base], [r0, r1, r2]]
        back_ps = [d_base, d_m0, d_m1]
        spare_ps = [r0, r2, c_ps[0]]

        ident_ok = sem("ident_ok")
        tables_in = sem("tables_in")
        tables_ok = sem("tables_ok")
        m2_in = [sem(f"m2_in{k}") for k in range(KT)]
        m2_diag, m2_hi_ok, m2_lo_ok = sem("m2_diag"), sem("m2_hi_ok"), sem("m2_lo_ok")
        m0_in = [sem("m0_in0"), sem("m0_in1")]
        m0_diag, m0_hi_ok, m0_lo_ok, m0_used = sem("m0_diag"), sem("m0_hi_ok"), sem("m0_lo_ok"), sem("m0_used")
        m2_used = sem("m2_used")
        bw_in = sem("bw_in")
        p_hi_ok, p_lo_ok = sem("p_hi_ok"), sem("p_lo_ok")
        a_in, a_hi_ok, a_lo_ok = sem("a_in"), sem("a_hi_ok"), sem("a_lo_ok")
        b2_in, b2_hi_ok, b2_lo_ok = sem("b2_in"), sem("b2_hi_ok"), sem("b2_lo_ok")
        q_in = [sem(f"q_in{k}") for k in range(KT)]
        q_diag, q_hi_ok, q_lo_ok = sem("q_diag"), sem("q_hi_ok"), sem("q_lo_ok")
        g_zero = sem("g_zero")
        x_ok, g_in, g_ok = sem("x_ok"), sem("g_in"), sem("g_ok")
        y_done, y_hi_ok, y_lo_ok = sem("y_done"), sem("y_hi_ok"), sem("y_lo_ok")
        v_done, low_ok = sem("v_done"), sem("low_ok")
        low_t_done, low_hi_ok, low_lo_ok = sem("low_t_done"), sem("low_hi_ok"), sem("low_lo_ok")
        lora_done, route, ex_ok, gated_ok = sem("lora_done"), sem("route"), sem("ex_ok"), sem("gated_ok")
        top_wait = sem("top_wait")
        gt_done, gt_hi_ok, gt_lo_ok = sem("gt_done"), sem("gt_hi_ok"), sem("gt_lo_ok")
        x3_done, x3n_ok = sem("x3_done"), sem("x3n_ok")
        x3t_done, x3t_hi_ok, x3t_lo_ok = sem("x3t_done"), sem("x3t_hi_ok"), sem("x3t_lo_ok")
        mask_ok = [sem(f"mask_ok{s}") for s in range(RING)]
        sign_even, sign_odd, slice_used = sem("sign_even"), sem("sign_odd"), sem("slice_used")
        bias_in, out_step, out_ok, stored = sem("bias_in"), sem("out_step"), sem("out_ok"), sem("stored")

        x_v = x.rearrange("(n b) c f -> n (b c) f", b=2)
        out_v = out.rearrange("(n b) c (h f) -> n h (b c) f", b=2, h=2)
        mask_v = mask.rearrange("(n b) (k p) (h f) -> n h k p b f", b=2, p=P, h=2)
        bias_v = bias.rearrange("(h a f) -> h a f", h=2, a=1)
        w0_v = w0.rearrange("(k p) (i c) -> i p k c", p=P, c=P)
        m2_v = m2ext.rearrange("(k p) n -> k p n", p=P)
        w3_v = w3t.rearrange("(k p) n -> k p n", p=P)
        bw_v = bw.rearrange("(k p) r -> p k r", p=P)

        def pair_of(view, t):
            return view[bass.ds(t, 1)]

        def y_half(yh):
            return yt[:, 4 * yh:4 * yh + 4]

        def in4(ps):
            return ps[:, :].rearrange("p (k n) -> p k n", k=4)

        def pair_a(tile):
            return tile[:, :, NEXT:NPV].rearrange("p k (b r) -> p b k r", b=2)

        q_first = [0, 1]
        q_at = {0: [2], 5: [3], 7: [4], 10: [5], 12: [6], 14: [7]}

        block = ctx.enter_context(nc.Block())

        @block.sync
        def _(sp):
            def load_x(t):
                sp.dma_start(x_in[:, :], pair_of(x_v, t).rearrange("a p f -> p (a f)")).then_inc(x_ok, 16)

            def load_g(t):
                for b in range(2):
                    c = sp.value_load(picks_sb[0:1, 0, bass.ds(2 * t + b, 1)], min_val=0, max_val=w1.shape[0] - 1)
                    sp.dma_start(g[TOK * b:TOK * b + TOK, TOK * b:TOK * b + TOK],
                                 w1[bass.ds(c, 1)].rearrange("a c d -> c (a d)")).then_inc(g_in, 16)

            def load_a(t):
                for b in range(2):
                    c = sp.value_load(picks_sb[0:1, 1, bass.ds(2 * t + b, 1)],
                                      min_val=0, max_val=labelers.shape[0] - 1)
                    sp.dma_start(a_raw[:, b, :, :].rearrange("p k r -> p (k r)"),
                                 labelers[bass.ds(c, 1)].rearrange("a p n -> p (a n)")).then_inc(a_in, 16)

            def load_mask(q, s):
                sp.dma_start(mask_in[:, s % RING, :, :],
                             pair_of(mask_v[:, s // KT, s % KT], q).rearrange("a p b f -> p (a b) f"))\
                    .then_inc(mask_ok[s % RING], 16)

            def load_bias(half, out_sb=out_sb):
                sp.dma_start(out_sb[:, :], bias_v[half].to_broadcast([P, HALF])).then_inc(bias_in, 16)

            def store(q, half, out_sb=out_sb):
                sp.dma_start(pair_of(out_v[:, half], q).rearrange("a p f -> p (a f)"), out_sb[:, :])\
                    .then_inc(stored, 16)

            sp.dma_start(m0_raw[0][:, :, :], w0_v[0]).then_inc(m0_in[0], 16)
            for k in range(KT):
                sp.dma_start(m2_raw[:, k, :], m2_v[k]).then_inc(m2_in[k], 16)
                if k == 0:
                    sp.dma_start(m0_raw[1][:, :, :], w0_v[1]).then_inc(m0_in[1], 16)
            sp.dma_start(bw_raw[:, :, :], bw_v).then_inc(bw_in, 16)
            sp.dma_start(b2_raw[:, :], b2).then_inc(b2_in, 16)
            sp.wait_ge(tables_in, 48)
            load_a(0)
            load_x(0)
            with sp.Fori(1, KT // 2) as i2:
                for j in range(2):
                    sp.wait_ge(m0_used, 2 * i2 + j - 1)
                    sp.dma_start(m0_raw[j][:, :, :],
                                 pair_of(w0_v, 2 * i2 + j).rearrange("a p k c -> p (a k) c")).then_inc(m0_in[j], 16)
            sp.wait_ge(g_zero, 1)
            load_g(0)
            load_bias(0)
            for s in range(4):
                load_mask(0, s)
            for k in range(KT):
                sp.wait_ge(m2_used, k + 1)
                sp.dma_start(q_raw[:, k, :], w3_v[k]).then_inc(q_in[k], 16)
                if k == 5:
                    sp.wait_ge(y_done, 2)
                    load_x(1)
                    load_g(1)
            sp.wait_ge(a_lo_ok, 1)
            load_a(1)
            for s in range(4, RING):
                load_mask(0, s)

            def iteration(t, prefetch, more):
                q = t - 1
                for s in range(STEPS):
                    if s == 0 and not more:
                        load_bias(1, last_out[1])
                    if s == 3 and prefetch:
                        sp.wait_ge(y_done, 2 * t + 2)
                        load_x(t + 1)
                        load_g(t + 1)
                        sp.wait_ge(a_lo_ok, t + 1)
                        load_a(t + 1)
                    if s < STEPS - RING or more:
                        sp.wait_ge(slice_used, STEPS * q + s + 1)
                        load_mask(q if s < STEPS - RING else q + 1, (s + RING) % STEPS)
                    if s == 9:
                        sp.wait_ge(out_ok, 2 * q + 2)
                        store(q, 0, out_sb if more else last_out[0])
                    if s == 11 and more:
                        sp.wait_ge(stored, 16 * (2 * q + 1))
                        load_bias(1)
                sp.wait_ge(out_ok, 2 * q + 3)
                store(q, 1, out_sb if more else last_out[1])
                if prefetch:
                    sp.wait_ge(stored, 16 * (2 * q + 2))
                    load_bias(0)
                elif more:
                    sp.wait_ge(y_done, 2 * t + 2)
                    load_bias(0, last_out[0])

            with sp.Fori(1, PAIRS - 1) as t:
                iteration(t, True, True)
            iteration(PAIRS - 1, False, True)
            iteration(PAIRS, False, False)
            sp.wait_ge(stored, 16 * 2 * PAIRS)

        @block.gpsimd
        def _(pool):
            nc.gpsimd.memset(ident[:, :], 0.0).then_inc(ident_ok, 1)
            nc.gpsimd.memset(g[:, :], 0.0).then_inc(g_zero, 1)
            pool.wait_ge(ident_ok, 1)
            nc.gpsimd.affine_select(out=ident[:, :], in_=ident[:, :], compare_op=ALU.not_equal, fill=1.0,
                                    base=0, pattern=[[-1, P]], channel_multiplier=1).then_inc(ident_ok, 1)

        @block.scalar
        def _(act):
            def hi(dst, src, scale=1.0):
                return nc.scalar.activation(dst, src, ACT.Copy, scale=scale)

            act.dma_start(picks_sb[:, :, :], picks.rearrange("(a i) n -> a i n", a=1)).then_inc(tables_in, 16)
            act.dma_start(lang_i[:, :], lang).then_inc(tables_in, 16)
            act.dma_start(coeff_sb[:, :], coeff).then_inc(tables_in, 16)
            for k in range(KT):
                if k < 2:
                    act.wait_ge(m0_diag, k + 1)
                    hi(m0_hi[k][:, :, :], m0_raw[k][:, :, :]).then_inc(m0_hi_ok, 1)
                act.wait_ge(m2_diag, k + 1)
                hi(m2_hi[:, k, :], m2_raw[:, k, :]).then_inc(m2_hi_ok, 1)

            def a_hi(t):
                act.wait_ge(a_in, 32 * (t + 1))
                if not (isinstance(t, int) and t == 0):
                    act.wait_ge(v_done, t)
                hi(pair_a(pv_hi), a_raw[:, :, :, :]).then_inc(a_hi_ok, 1)

            a_hi(0)
            act.wait_ge(b2_in, 16)
            hi(b2_hi[:, :], b2_raw[:, :]).then_inc(b2_hi_ok, 1)

            def p_hi(i, j):
                act.wait_ge(m0_used, i + 1)
                for c in range(3):
                    w = cuts[c + 1] - cuts[c]
                    dst = pv_hi[:, bass.ds(i, 1), cuts[c]:cuts[c + 1]].rearrange("p a n -> p (a n)")
                    hi(dst, set_ps[j][c][:, 0:w]).then_inc(p_hi_ok, 1)

            with act.Fori(0, KT // 2 - 1) as i2:
                for j in range(2):
                    p_hi(2 * i2 + j, j)
                    act.wait_ge(m0_diag, 2 * i2 + j + 3)
                    hi(m0_hi[j][:, :, :], m0_raw[j][:, :, :]).then_inc(m0_hi_ok, 1)
            p_hi(KT - 2, 0)
            act.wait_ge(bw_in, 16)
            for c in range(3):
                ins = hi(m0_hi[0][:, :, RL * c:RL * c + RL], bw_raw[:, :, :], scale=0.5)
            ins.then_inc(m0_hi_ok, 1)
            p_hi(KT - 1, 1)

            def y_hi(t, yh, ps):
                act.wait_ge(y_done, 2 * t + yh + 1)
                hi(y_half(yh)[:, :, 0, :], in4(ps)).then_inc(y_hi_ok, 1)

            def q_upper(k):
                act.wait_ge(q_diag, k + 1)
                hi(q_hi[:, k, :], q_raw[:, k, :]).then_inc(q_hi_ok, 1)

            def to_sign(q, s):
                act.wait_ge(mask_ok[s % RING], 16 * (2 * q + s // RING + 1))
                nc.scalar.activation(sign[:, s % RING, :, :], mask_in[:, s % RING, :, :], ACT.Copy,
                                     scale=2.0, bias=-1.0).then_inc(sign_odd, 1)

            for s in range(1, AHEAD, 2):
                to_sign(0, s)
            y_hi(0, 0, r2)
            y_hi(0, 1, r0)
            for k in q_first:
                q_upper(k)
            act.wait_ge(m2_used, KT)
            for c in range(3):
                w = cuts[c + 1] - cuts[c]
                hi(bs[:, cuts[c]:cuts[c + 1]], set_ps[0][c][:, 0:w]).then_inc(p_hi_ok, 1)

            def x3t_hi(t, h):
                act.wait_ge(x3t_done, 2 * t + h + 1)
                hi(x3t[:, 4 * h:4 * h + 4, 1:3, :],
                   r1[:, :].rearrange("p (k b n) -> p k b n", k=4, b=2)).then_inc(x3t_hi_ok, 1)

            def x3_out(t, h):
                act.wait_ge(x3_done, 2 * t + h + 1)
                if h == 1:
                    act.wait_ge(x3t_done, 2 * t + 1)
                if h == 0:
                    nc.scalar.activation(x3n[:, :], c_ps[0][:, :], ACT.Copy).then_inc(x3n_ok, 1)
                else:
                    nc.scalar.activation(x3n[:, 0:HALF - PX], c_ps[1][:, 0:HALF - PX], ACT.Copy)
                    nc.scalar.activation(x3n[:, HALF - PX:HALF], r0[:, 0:PX], ACT.Copy).then_inc(x3n_ok, 1)

            def iteration(t, front, back, prefetch, more):
                q = t - 1
                if front and back:
                    y_hi(t, 0, r2)
                    x3t_hi(q, 1)
                    y_hi(t, 1, r0)
                for s in range(STEPS):
                    if back and s % 2 == 1 and (s + AHEAD < STEPS or more):
                        to_sign(q if s + AHEAD < STEPS else q + 1, (s + AHEAD) % STEPS)
                    if front and s == 6:
                        act.wait_ge(low_t_done, t + 1)
                        hi(low_t[:, :], r1[:, 0:P]).then_inc(low_hi_ok, 1)
                    if prefetch and s == 7:
                        a_hi(t + 1)
                    if front and s == 9:
                        act.wait_ge(route, 11 * t + 2)
                        nc.scalar.activation(ex[:, :], top[:, 0:1], ACT.Exp, scale=-1.0, bias=top[:, 1:2])\
                            .then_inc(ex_ok, 1)
                    if front and s == 12:
                        act.wait_ge(gt_done, t + 1)
                        hi(gt_hi[:, :], r2[:, 0:P]).then_inc(gt_hi_ok, 1)
                    if front and s == 13:
                        x3_out(t, 0)
                    if front and s == 15:
                        x3t_hi(t, 0)
                    if back and not front and s == 3:
                        x3t_hi(q, 1)
                    for k in q_at.get(s, []) if not back else []:
                        q_upper(k)
                if front:
                    x3_out(t, 1)

            iteration(0, True, False, True, True)
            with act.Fori(1, PAIRS - 1) as t:
                iteration(t, True, True, True, True)
            iteration(PAIRS - 1, True, True, False, True)
            iteration(PAIRS, False, True, False, False)

        @block.vector
        def _(dve):
            def lo(dst, src, hi_part):
                return nc.vector.tensor_tensor(dst, src, hi_part.bitcast(F32), ALU.subtract)

            def add_diag(tile):
                return nc.vector.tensor_tensor(tile, tile, ident[:, :], ALU.add)

            dve.sem_inc(out_ok, 1)
            dve.wait_ge(ident_ok, 2)

            def m0_diagonal(i):
                dve.wait_ge(m0_in[i], 16)
                add_diag(m0_raw[i][:, i, :]).then_inc(m0_diag, 1)

            def m0_lower(i):
                dve.wait_ge(m0_hi_ok, i + 1)
                lo(m0_lo[i][:, :, :], m0_raw[i][:, :, :], m0_hi[i][:, :, :]).then_inc(m0_lo_ok, 1)

            def m2_diagonal(k):
                dve.wait_ge(m2_in[k], 16)
                add_diag(m2_raw[:, k, P * k:P * k + P]).then_inc(m2_diag, 1)

            m0_diagonal(0)
            m2_diagonal(0)
            m0_lower(0)
            m0_diagonal(1)
            for k in range(KT):
                if k + 1 < KT:
                    m2_diagonal(k + 1)
                dve.wait_ge(m2_hi_ok, k + 1)
                lo(m2_lo[:, k, :], m2_raw[:, k, :], m2_hi[:, k, :]).then_inc(m2_lo_ok, 1)
                if k == 0:
                    m0_lower(1)

            def a_lo(t):
                dve.wait_ge(a_hi_ok, t + 1)
                lo(pair_a(pv_lo), a_raw[:, :, :, :], pair_a(pv_hi)).then_inc(a_lo_ok, 1)

            a_lo(0)
            dve.wait_ge(b2_hi_ok, 1)
            lo(b2_lo[:, :], b2_raw[:, :], b2_hi[:, :]).then_inc(b2_lo_ok, 1)

            dve.wait_ge(tables_in, 48)
            nc.vector.tensor_copy(lang_f[:, :], lang_i[:, :]).then_inc(tables_ok, 1)
            for e in range(E):
                nc.vector.memset(iota[:, e:e + 1], float(e)).then_inc(tables_ok, 1)
            dve.wait_ge(tables_ok, 1)
            for e in range(E):
                nc.vector.tensor_scalar(lang_hot[:, :, e], lang_f[:, :], float(e), LANG_BIAS,
                                        ALU.is_equal, ALU.mult).then_inc(tables_ok, 1)
            TABLES = 1 + 2 * E

            def p_lo(i, j):
                for c in range(3):
                    w = cuts[c + 1] - cuts[c]
                    dve.wait_ge(p_hi_ok, 3 * i + c + 1)
                    at_lo = pv_lo[:, bass.ds(i, 1), cuts[c]:cuts[c + 1]].rearrange("p a n -> p (a n)")
                    at_hi = pv_hi[:, bass.ds(i, 1), cuts[c]:cuts[c + 1]].rearrange("p a n -> p (a n)")
                    lo(at_lo, set_ps[j][c][:, 0:w], at_hi).then_inc(p_lo_ok, 1)

            with dve.Fori(0, KT // 2 - 1) as i2:
                for j in range(2):
                    p_lo(2 * i2 + j, j)
                    dve.wait_ge(m0_in[j], 16 * (i2 + 2))
                    add_diag(m0_raw[j][:, bass.ds(2 * i2 + j + 2, 1), :].rearrange("p a n -> p (a n)"))\
                        .then_inc(m0_diag, 1)
                    dve.wait_ge(m0_hi_ok, 2 * i2 + j + 3)
                    lo(m0_lo[j][:, :, :], m0_raw[j][:, :, :], m0_hi[j][:, :, :]).then_inc(m0_lo_ok, 1)
            p_lo(KT - 2, 0)
            dve.wait_ge(m0_hi_ok, KT + 1)
            nc.vector.scalar_tensor_tensor(out=m0_hi[0][:, :, 3 * RL:], in0=bw_raw[:, :, :], scalar=0.5,
                                           in1=m0_hi[0][:, :, 0:RL].bitcast(F32),
                                           op0=ALU.mult, op1=ALU.subtract).then_inc(m0_lo_ok, 1)

            def make_g(t):
                dve.wait_ge(g_in, 32 * (t + 1))
                add_diag(g[:, :]).then_inc(g_ok, 1)

            def y_lo(t, yh, ps):
                dve.wait_ge(y_hi_ok, 2 * t + yh + 1)
                lo(y_half(yh)[:, :, 1, :], in4(ps), y_half(yh)[:, :, 0, :]).then_inc(y_lo_ok, 1)

            dve.wait_ge(tables_ok, TABLES)
            make_g(0)
            p_lo(KT - 1, 1)
            def to_sign(q, s):
                dve.wait_ge(mask_ok[s % RING], 16 * (2 * q + s // RING + 1))
                nc.vector.tensor_scalar(sign[:, s % RING, :, :], mask_in[:, s % RING, :, :], 2.0, -1.0,
                                        ALU.mult, ALU.add).then_inc(sign_even, 1)

            def q_diagonal(k):
                dve.wait_ge(q_in[k], 16)
                add_diag(q_raw[:, k, P * k:P * k + P]).then_inc(q_diag, 1)

            def q_lower(k):
                if k + 1 < KT:
                    q_diagonal(k + 1)
                dve.wait_ge(q_hi_ok, k + 1)
                lo(q_lo[:, k, :], q_raw[:, k, :], q_hi[:, k, :]).then_inc(q_lo_ok, 1)

            for s in range(0, AHEAD, 2):
                to_sign(0, s)
            y_lo(0, 0, r2)
            y_lo(0, 1, r0)
            q_diagonal(0)
            for k in q_first:
                q_lower(k)
            for c in range(3):
                w = cuts[c + 1] - cuts[c]
                dve.wait_ge(p_hi_ok, 3 * KT + c + 1)
                rows = bs[RL:2 * RL, cuts[c]:cuts[c + 1]]
                lo(rows, set_ps[0][c][RL:2 * RL, 0:w], rows).then_inc(p_lo_ok, 1)

            def x3t_lo(t, h):
                dve.wait_ge(x3t_hi_ok, 2 * t + h + 1)
                tiles = slice(4 * h, 4 * h + 4)
                ps = r1[:, :].rearrange("p (k b n) -> p k b n", k=4, b=2)
                lo(x3t[:, tiles, 0:4:3, :], ps, x3t[:, tiles, 1:3, :])
                lo(x3t[:, tiles, 4:6, :], ps, x3t[:, tiles, 1:3, :]).then_inc(x3t_lo_ok, 1)

            def pick_low(t):
                dve.wait_ge(v_done, t + 1)
                for b in range(2):
                    mine = slice(TOK * b, TOK * b + TOK)
                    cols = r0[mine, LOW0 + RL * b:LOW0 + RL * b + RL]
                    nc.vector.tensor_copy(low[mine, :, :], cols.unsqueeze(1).to_broadcast([TOK, 4, RL]))\
                        .then_inc(low_ok, 1)

            def route_top(t):
                dve.wait_ge(lora_done, t + 1)
                nc.vector.tensor_tensor(logits[:, :], r0[:, PX:A0],
                                        lang_hot[:, bass.ds(t, 1), :].rearrange("p a e -> p (a e)"), ALU.add)\
                    .then_inc(route, 1)
                dve.wait_ge(route, 11 * t + 1).then_inc(top_wait, 1)
                nc.vector.max(top[:, :], logits[:, :]).then_inc(route, 1)
                dve.wait_ge(route, 11 * t + 2).then_inc(top_wait, 1)
                nc.vector.max_index(top_at[:, :], top[:, :], logits[:, :]).then_inc(route, 1)
                dve.wait_ge(route, 11 * t + 3)
                nc.vector.tensor_copy(top_f[:, :], top_at[:, 0:2]).then_inc(route, 1)

            def route_gates(t):
                dve.wait_ge(ex_ok, t + 1)
                nc.vector.tensor_scalar(den[:, :], ex[:, :], 1.0, None, ALU.add).then_inc(route, 1)
                dve.wait_ge(route, 11 * t + 5)
                nc.vector.reciprocal(rden[:, :], den[:, :]).then_inc(route, 1)
                dve.wait_ge(route, 11 * t + 6)
                nc.vector.tensor_scalar(w_a[:, :], rden[:, :], 2.0, None, ALU.mult).then_inc(route, 1)
                nc.vector.tensor_scalar(w_b[:, :], rden[:, :], ex[:, 0:1], 2.0, ALU.mult, ALU.mult)\
                    .then_inc(route, 1)
                dve.wait_ge(route, 11 * t + 8)
                nc.vector.tensor_scalar(gate_a[:, :], iota[:, :], top_f[:, 0:1], w_a[:, 0:1],
                                        ALU.is_equal, ALU.mult).then_inc(route, 1)
                nc.vector.tensor_scalar(gate_b[:, :], iota[:, :], top_f[:, 1:2], w_b[:, 0:1],
                                        ALU.is_equal, ALU.mult).then_inc(route, 1)
                dve.wait_ge(route, 11 * t + 10)
                nc.vector.tensor_tensor(gates[:, :], gate_a[:, :], gate_b[:, :], ALU.add).then_inc(route, 1)
                dve.wait_ge(route, 11 * t + 11)
                nc.vector.tensor_tensor(gated[:, :, :], r0[:, A0:LOW0].rearrange("p (e r) -> p e r", e=E),
                                        gates[:, :].unsqueeze(2).to_broadcast([P, E, R]), ALU.mult)\
                    .then_inc(gated_ok, 1)

            def finish_half(q, h, banks, out_sb):
                n = 4 * (2 * q + h)
                dve.wait_ge(slice_used, STEPS * q + KT * (h + 1))
                dve.wait_ge(bias_in, 16 * (2 * q + h + 1))
                nc.vector.tensor_tensor(out_sb[:, :], banks[0][:, :], out_sb[:, :], ALU.add).then_inc(out_step, 1)
                for part in range(2):
                    for b, ps in enumerate(banks[1:]):
                        mine = slice(TOK * b, TOK * b + TOK)
                        if b == 0:
                            dve.wait_ge(out_step, n + (1 if part == 0 else 2))
                        elif part == 1:
                            dve.wait_ge(out_step, n + 3)
                        ins = nc.vector.scalar_tensor_tensor(
                            out=out_sb[mine, :], in0=ps[TOK * part:TOK * part + TOK, :],
                            scalar=coeff_sb[mine, bass.ds(q, 1)], in1=out_sb[mine, :],
                            op0=ALU.mult, op1=ALU.add)
                        if part == 1 and b == 1:
                            ins.then_inc(out_ok, 1)
                        else:
                            ins.then_inc(out_step, 1)

            def iteration(t, front, back, prefetch, more):
                q = t - 1
                if front and back:
                    y_lo(t, 0, r2)
                    x3t_lo(q, 1)
                    y_lo(t, 1, r0)
                for s in range(STEPS):
                    if back and s % 2 == 0 and (s + AHEAD < STEPS or more):
                        to_sign(q if s + AHEAD < STEPS else q + 1, (s + AHEAD) % STEPS)
                    if front and s == 4:
                        pick_low(t)
                    if front and s == 6:
                        dve.wait_ge(low_hi_ok, t + 1)
                        rows = low_t[2 * RL:3 * RL, :]
                        lo(rows, r1[2 * RL:3 * RL, 0:P], rows).then_inc(low_lo_ok, 1)
                    if back and s == 7:
                        finish_half(q, 0, *((back_ps, out_sb) if front else (spare_ps, last_out[0])))
                    if front and s == 8:
                        route_top(t)
                    if front and s == 9:
                        route_gates(t)
                    if front and s == 12:
                        dve.wait_ge(gt_hi_ok, t + 1)
                        lo(gt_lo[:, :], r2[:, 0:P], gt_hi[:, :]).then_inc(gt_lo_ok, 1)
                    if prefetch and s == 11:
                        a_lo(t + 1)
                    if prefetch and s == 13:
                        make_g(t + 1)
                    if front and s == 15:
                        x3t_lo(t, 0)
                    if back and not front and s == 3:
                        x3t_lo(q, 1)
                    for k in q_at.get(s, []) if not back else []:
                        q_lower(k)
                if back:
                    finish_half(q, 1, back_ps, out_sb if front else last_out[1])

            iteration(0, True, False, True, True)
            with dve.Fori(1, PAIRS - 1) as t:
                iteration(t, True, True, True, True)
            iteration(PAIRS - 1, True, True, False, True)
            iteration(PAIRS, False, True, False, False)

        @block.tensor
        def _(pe):
            mm = nc.tensor.matmul

            def setup_step(j, k, arriving=False):
                hi_t, lo_t = m0_hi[j], m0_lo[j]
                for n, (a, b) in enumerate(((hi_t, m2_hi), (lo_t, m2_hi), (hi_t, m2_lo))):
                    if arriving and n == 0:
                        pe.wait_ge(m0_hi_ok, j + 1)
                        pe.wait_ge(m2_hi_ok, k + 1)
                    elif arriving and n == 1:
                        pe.wait_ge(m0_lo_ok, j + 1)
                    elif arriving:
                        pe.wait_ge(m2_lo_ok, k + 1)
                    for c in range(3):
                        w = cuts[c + 1] - cuts[c]
                        ins = mm(set_ps[j][c][:, 0:w], a[:, k, :], b[:, k, cuts[c]:cuts[c + 1]],
                                 start=(k == 0 and n == 0), stop=(k == KT - 1 and n == 2))
                if k == KT - 1:
                    ins.then_inc(m0_used, 1)

            ahead = iter(range(KT))
            for k in range(KT):
                setup_step(0, k, True)
                if k % 2 == 1:
                    setup_step(1, next(ahead), True)
            for k in ahead:
                setup_step(1, k, True)
            with pe.Fori(1, KT // 2) as i2:
                for j in range(2):
                    pe.wait_ge(m0_lo_ok, 2 * i2 + j + 1)
                    pe.wait_ge(p_lo_ok, 3 * (2 * i2 + j - 1))
                    for k in range(KT):
                        setup_step(j, k)

            def low_rank_step(k):
                for c in range(3):
                    w = cuts[c + 1] - cuts[c]
                    mm(set_ps[0][c][:, 0:w], m0_hi[0][:, k, :], m2_hi[:, k, cuts[c]:cuts[c + 1]],
                       start=(k == 0), stop=(k == KT - 1), skip_group_check=True)
                for c in range(3):
                    w = cuts[c + 1] - cuts[c]
                    ins = mm(set_ps[0][c][0:3 * RL, 0:w], m0_hi[0][:, k, 0:3 * RL],
                             m2_lo[:, k, cuts[c]:cuts[c + 1]], start=False, stop=(k == KT - 1),
                             skip_group_check=True)
                ins.then_inc(m2_used, 1)

            def y_part(t, yh, ps):
                if yh == 0:
                    pe.wait_ge(x_ok, 16 * (t + 1))
                    pe.wait_ge(g_ok, t + 1)
                for k in range(4):
                    n = P * (4 * yh + k)
                    ins = mm(ps[:, P * k:P * k + P], x_in[:, n:n + P], g[:, :], start=True, stop=True)
                ins.then_inc(y_done, 1)

            def v_step(t, k):
                if k == 0:
                    pe.wait_ge(y_lo_ok, 2 * t + 2)
                    pe.wait_ge(a_lo_ok, t + 1)
                for n, (a, b) in enumerate(((0, pv_hi), (0, pv_lo), (1, pv_hi))):
                    ins = mm(r0[:, 0:NV], yt[:, k, a, :], b[:, k, V0:NPV],
                             start=(k == 0 and n == 0), stop=(k == KT - 1 and n == 2), skip_group_check=True)
                if k == KT - 1:
                    ins.then_inc(v_done, 1)

            def low_turn(t):
                pe.wait_ge(low_ok, 2 * t + 2)
                if not (isinstance(t, int) and t == 0):
                    pe.wait_ge(x3t_lo_ok, 2 * t)
                nc.tensor.transpose(r1[:, 0:P], low[:, :, :].rearrange("p c r -> p (c r)"), ident[:, :])\
                    .then_inc(low_t_done, 1)

            def lora(t):
                pe.wait_ge(low_lo_ok, t + 1)
                mm(r0[:, 0:LOW0], low_t[:, :], bs[:, V0:NEXT], start=False, stop=True,
                   skip_group_check=True).then_inc(lora_done, 1)

            def x3_step(t, h, k):
                cols = slice(HALF * h, min(HALF * h + HALF, V0))
                n_cols = cols.stop - cols.start
                if isinstance(t, int) and t == 0 and k == 0:
                    pe.wait_ge(p_lo_ok, 3 * (KT + 1))
                for n, (a, b) in enumerate(((0, pv_hi), (0, pv_lo), (1, pv_hi))):
                    mm(c_ps[h][:, 0:n_cols], yt[:, k, a, :], b[:, k, cols], start=(k == 0 and n == 0), stop=False)

            def x3_tail(t, h):
                pe.wait_ge(gt_lo_ok, t + 1)
                gated_passes = ((gt_hi, b2_hi), (gt_hi, b2_lo), (gt_lo, b2_hi))
                if h == 1:
                    for n, (a, b) in enumerate(gated_passes):
                        mm(r0[:, 0:PX], a[:, :], b[:, V0:D], start=False, stop=(n == 2), skip_group_check=True)
                cols = slice(HALF * h, min(HALF * h + HALF, V0))
                ps = c_ps[h][:, 0:cols.stop - cols.start]
                mm(ps, low_t[:, :], bs[:, cols], start=False, stop=False)
                for n, (a, b) in enumerate(gated_passes):
                    ins = mm(ps, a[:, :], b[:, cols], start=False, stop=(n == 2))
                ins.then_inc(x3_done, 1)

            def turn_gated(t):
                pe.wait_ge(gated_ok, t + 1)
                nc.tensor.transpose(r2[:, 0:P], gated[:, :, :].rearrange("p e r -> p (e r)"), ident[:, :])\
                    .then_inc(gt_done, 1)

            def turn_x3(t, h):
                pe.wait_ge(x3n_ok, 2 * t + h + 1)
                if h == 1:
                    pe.wait_ge(x3t_lo_ok, 2 * t + 1)
                for k in range(4):
                    ins = nc.tensor.transpose(r1[:, P * k:P * k + P], x3n[:, P * k:P * k + P], ident[:, :])
                ins.then_inc(x3t_done, 1)

            def back_step(q, s, banks):
                h, k = s // KT, s % KT
                cols = slice(HALF * h, HALF * h + HALF)
                if s == 0 and banks is back_ps:
                    pe.wait_ge(out_ok, 2 * q + 1)
                elif s == KT:
                    pe.wait_ge(out_ok, 2 * q + (2 if isinstance(q, bass.RuntimeValue) or q < PAIRS - 1 else 1))
                if s == 0 or s == 4:
                    pe.wait_ge(x3t_lo_ok, 2 * q + s // 4 + 1)
                pe.wait_ge(sign_even if s % 2 == 0 else sign_odd, STEPS // 2 * q + s // 2 + 1)
                for b, ps in enumerate(banks[1:]):
                    mm(ps[:, :], x3t[:, k, 2 * b:2 * b + 2, :].rearrange("p l n -> p (l n)"), sign[:, s % RING, b, :],
                       start=(k == 0), stop=(k == KT - 1))
                if s == 0 and banks is spare_ps:
                    pe.wait_ge(x3n_ok, 2 * PAIRS)
                for n, (a, b) in enumerate(((1, q_hi), (1, q_lo), (4, q_hi))):
                    ins = mm(banks[0][:, :], x3t[:, k, a:a + 2, :].rearrange("p b n -> p (b n)"), b[:, k, cols],
                             start=(k == 0 and n == 0), stop=(k == KT - 1 and n == 2))
                ins.then_inc(slice_used, 1)

            fill = [
                [], [("v", 0), ("v", 1), ("v", 2)], [("v", 3), ("v", 4), ("v", 5)], [("v", 6), ("v", 7)],
                [("x3", 0, 0)], [("low",), ("x3", 0, 1)], [("x3", 0, 2)],
                [("lora",), ("x3", 0, 3), ("x3", 0, 4), ("x3", 0, 5), ("x3", 0, 6), ("x3", 0, 7), ("x3", 1, 0)],
                [("x3", 1, 1)], [("x3", 1, 2)], [("x3", 1, 3)], [("gated",), ("x3", 1, 4)],
                [("tail", 0)], [("x3", 1, 5)], [("turn", 0)], [("x3", 1, 6), ("x3", 1, 7), ("tail", 1)],
            ]
            alone = [("v", k) for k in range(KT)] + [("x3", 0, k) for k in range(3)] + [("low",)]
            alone += [("x3", 0, k) for k in range(3, 6)] + [("lora",), ("x3", 0, 6), ("x3", 0, 7)]
            alone += [("x3", 1, k) for k in range(6)] + [("gated",), ("x3", 1, 6), ("tail", 0), ("x3", 1, 7)]
            alone += [("tail", 1), ("turn", 0)]

            def front_work(t, item):
                kind = item[0]
                if kind == "v":
                    v_step(t, item[1])
                elif kind == "low":
                    low_turn(t)
                elif kind == "lora":
                    lora(t)
                elif kind == "x3":
                    x3_step(t, item[1], item[2])
                elif kind == "gated":
                    turn_gated(t)
                elif kind == "tail":
                    x3_tail(t, item[1])
                else:
                    turn_x3(t, item[1])

            def iteration(t, front):
                q = t - 1
                if front:
                    y_part(t, 0, r2)
                    turn_x3(q, 1)
                    y_part(t, 1, r0)
                for s in range(STEPS):
                    back_step(q, s, spare_ps if not front and s < KT else back_ps)
                    if front:
                        for item in fill[s]:
                            front_work(t, item)
                    elif s == 3:
                        turn_x3(q, 1)

            pe.wait_ge(m0_lo_ok, KT + 1)
            pe.wait_ge(p_lo_ok, 3 * (KT - 1))
            for k in range(KT):
                low_rank_step(k)
                if k == 3:
                    pe.wait_ge(ident_ok, 2)
                    pe.wait_ge(p_lo_ok, 3 * KT)
                    y_part(0, 0, r2)
                    y_part(0, 1, r0)
            pe.wait_ge(b2_lo_ok, 1)
            for item in alone:
                front_work(0, item)
            pe.wait_ge(q_lo_ok, KT)
            with pe.Fori(1, PAIRS) as t:
                iteration(t, True)
            iteration(PAIRS, False)


def kernel(**inputs):
    import numpy as np
    import concourse.bacc as bacc
    from concourse.bass_utils import run_bass_kernel_spmd

    def arr(name):
        return np.asarray(inputs[name])

    x = arr("x")
    pairs = x.shape[0] // 2

    def per_token(a):
        return np.repeat(a.reshape(pairs, 2).T, 64, axis=0)

    expert_a = arr("L2_cond_A")
    expert_b = arr("L2_cond_B")
    labeler_a = arr("L0_cond_lora_A")
    nl, d, rank = labeler_a.shape
    arrays = {
        "x": x,
        "picks": np.stack([arr("itok_B_0_15"), arr("itok_B_0_2")]),
        "lang": per_token(arr("itok_B_0_7")),
        "coeff": per_token(arr("condB_coeff")),
        "mask": arr("mask_Bx4096x4096_ik1"),
        "w0": arr("L0_cond_W"),
        "bw": arr("L0_cond_lora_B_w"),
        "labelers": labeler_a.reshape(nl, d // 128, 128, rank).transpose(0, 2, 1, 3).reshape(nl, 128, -1),
        "m2ext": np.concatenate([arr("L2_cond_W").T, arr("L2_cond_Wr").T, expert_a.reshape(-1, d).T], axis=1),
        "b2": expert_b.transpose(0, 2, 1).reshape(-1, d),
        "w3t": arr("L3_cond_W").T,
        "w1": arr("L1_cond_weights"),
        "bias": arr("L3_cond_b"),
    }
    nc = bacc.Bacc("TRN2", target_bir_lowering=False, num_devices=1, dynamic_dma_scratch_size=SCRATCH)
    feed, args = {}, {}
    for name, a in arrays.items():
        a = np.ascontiguousarray(a)
        feed[f"in_{name}"] = a
        args[name] = nc.dram_tensor(f"in_{name}", a.shape, mybir.dt.from_np(a.dtype), kind="ExternalInput").ap()
    args["out"] = nc.dram_tensor("out_x", x.shape, F32, kind="ExternalOutput").ap()
    layers_kernel(nc, **args)
    result = run_bass_kernel_spmd(nc, [feed], core_ids=[0])
    return result.results[0]["out_x"]
```

```python
from contextlib import ExitStack

import concourse.bass as bass
from concourse import mybir

F32 = mybir.dt.float32
F32R = mybir.dt.float32r
BF16 = mybir.dt.bfloat16
I32 = mybir.dt.int32
U32 = mybir.dt.uint32
ALU = mybir.AluOpType
ACT = mybir.ActivationFunctionType
AX = mybir.AxisListType

P = 128
SCRATCH = 1024


def layers_kernel(nc, x, picks, lang, coeff, mask, w0, bw, labelers, m2ext, b2, w3t, w1, bias, out):
    NB, TOK, D = x.shape
    PAIRS = NB // 2
    KT = D // P
    HALF = D // 2
    NEXT = m2ext.shape[1]
    E = 8
    R = (NEXT - D - E) // E
    ER = E * R
    RL = bw.shape[1]
    NPV = NEXT + 2 * RL
    NV = 256
    V0 = NPV - NV
    PX = D - V0
    A0 = PX + E
    LOW0 = A0 + ER
    STEPS = 2 * KT
    RING = 8
    AHEAD = 4
    FIRST = 2
    LANG_BIAS = 5.0
    cuts = [0, 388, 774, NEXT]
    assert NEXT == 1160 and NPV == 1224 and ER == P and 4 * RL == P and STEPS == 16

    base = nc.sbuf_base + (-nc.sbuf_base) % 32
    place = [base]

    def at(name, shape, dt, offset=None):
        if offset is None:
            offset = place[0]
            size = 2 if dt == BF16 else 4
            for n in shape[1:]:
                size *= n
            place[0] += size + (-size) % 32
        return nc.alloc_sbuf_tensor_at(name, shape, dt, offset=offset), offset

    pv_hi, o_pv = at("pv_hi", [P, KT, NPV], F32R)
    pv_lo, _ = at("pv_lo", [P, KT, NPV], F32R)
    last_sign, _ = at("last_sign", [P, 2, KT, NPV], F32R, o_pv)
    last_mask, _ = at("last_mask", [P, 2, KT, NPV], I32, o_pv)
    bs, _ = at("bs", [P, NEXT], F32R)
    q_lo, o_m2 = at("q_lo", [P, KT, D], F32R)
    q_raw, _ = at("q_raw", [P, KT, D], F32, o_m2)
    x3n, _ = at("x3n", [P, HALF], F32)
    gated, _ = at("gated", [P, E, R], F32)
    low, _ = at("low", [P, 4, RL], F32)
    gt_hi, _ = at("gt_hi", [P, P], F32R)
    gt_lo, _ = at("gt_lo", [P, P], F32R)
    o_m2_lo = o_m2 + 4 * KT * NEXT
    assert place[0] <= o_m2_lo
    place[0] = o_m2_lo
    q_hi, _ = at("q_hi", [P, KT, D], F32R)
    x3t, _ = at("x3t", [P, KT, 6, TOK], F32R)
    m2_hi, _ = at("m2_hi", [P, KT, NEXT], F32R, o_m2)
    m2_lo, _ = at("m2_lo", [P, KT, NEXT], F32R, o_m2_lo)
    m2_raw, _ = at("m2_raw", [P, KT, NEXT], F32, o_m2_lo)
    assert o_m2_lo + 4 * KT * NEXT <= place[0]
    b2_hi, _ = at("b2_hi", [P, D], F32R)
    b2_lo, o = at("b2_lo", [P, D], F32R)
    b2_raw, _ = at("b2_raw", [P, D], F32, o)
    x_in, o = at("x_in", [P, D], F32)
    last_out = [at(f"last_out{h}", [P, HALF], F32, o + 4 * HALF * h)[0] for h in range(2)]
    yt, o_yt = at("yt", [P, KT, 2, P], F32R)
    bw_raw, _ = at("bw_raw", [P, KT, RL], F32, o_yt)
    out_sb, _ = at("out_sb", [P, HALF], F32)
    sign, o_ring = at("sign", [P, RING, 2, HALF], F32R)
    mask_in, _ = at("mask_in", [P, RING, 2, HALF], I32, o_ring)
    m0_hi, m0_lo, m0_raw = [], [], []
    for b in range(2):
        o = o_ring + 4 * D * (4 + 2 * b)
        m0_hi.append(at(f"m0_hi{b}", [P, KT, P], F32R, o)[0])
        m0_lo.append(at(f"m0_lo{b}", [P, KT, P], F32R, o + 4 * D)[0])
        m0_raw.append(at(f"m0_raw{b}", [P, KT, P], F32, o + 4 * D)[0])
    ident, _ = at("ident", [P, P], F32)
    g, _ = at("g", [P, P], F32)
    a_raw, _ = at("a_raw", [P, 2, KT, RL], F32)
    low_t, _ = at("low_t", [P, P], F32R)
    picks_sb, _ = at("picks_sb", [1, 2, NB], I32)
    lang_i, _ = at("lang_i", [P, PAIRS], I32)
    lang_f, _ = at("lang_f", [P, PAIRS], F32)
    coeff_sb, _ = at("coeff_sb", [P, PAIRS], F32)
    lang_hot, _ = at("lang_hot", [P, PAIRS, E], BF16)
    iota, _ = at("iota", [P, E], F32)
    logits, _ = at("logits", [P, E], F32)
    top, _ = at("top", [P, E], F32)
    top_at, _ = at("top_at", [P, E], U32)
    top_f, _ = at("top_f", [P, 2], F32)
    ex, _ = at("ex", [P, 1], F32)
    den, _ = at("den", [P, 1], F32)
    rden, _ = at("rden", [P, 1], F32)
    w_a, _ = at("w_a", [P, 1], F32)
    w_b, _ = at("w_b", [P, 1], F32)
    gate_a, _ = at("gate_a", [P, E], F32)
    gate_b, _ = at("gate_b", [P, E], F32)
    gates, _ = at("gates", [P, E], F32)
    assert place[0] <= nc.sbuf_top, place[0]

    ctx = ExitStack()
    with ctx:
        def bank(name):
            return ctx.enter_context(nc.psum_tensor(name, [P, 512], F32))

        def sem(name):
            return ctx.enter_context(nc.semaphore(name))

        r0, r1, r2 = bank("r0"), bank("r1"), bank("r2")
        c_ps = [bank("c0"), bank("c1")]
        d_base, d_m0, d_m1 = bank("d_base"), bank("d_m0"), bank("d_m1")
        set_ps = [[c_ps[0], c_ps[1], d_base], [r0, r1, r2]]
        back_ps = [d_base, d_m0, d_m1]
        spare_ps = [c_ps[0], r2, r0]

        ident_ok = sem("ident_ok")
        tables_in = sem("tables_in")
        tables_ok = sem("tables_ok")
        m2_in = [sem(f"m2_in{k}") for k in range(KT)]
        m2_diag, m2_hi_ok, m2_lo_ok = sem("m2_diag"), sem("m2_hi_ok"), sem("m2_lo_ok")
        m0_in = [sem("m0_in0"), sem("m0_in1")]
        first_in, first_diag, first_hi_ok, first_lo_ok = (sem(n) for n in ("first_in", "first_diag", "first_hi_ok",
                                                                           "first_lo_ok"))
        m0_diag, m0_hi_ok, m0_lo_ok, m0_used = sem("m0_diag"), sem("m0_hi_ok"), sem("m0_lo_ok"), sem("m0_used")
        m2_used = sem("m2_used")
        bw_in = sem("bw_in")
        p_hi_ok, p_lo_ok = sem("p_hi_ok"), sem("p_lo_ok")
        a_in, a_hi_ok, a_lo_ok = sem("a_in"), sem("a_hi_ok"), sem("a_lo_ok")
        b2_in, b2_hi_ok, b2_lo_ok = sem("b2_in"), sem("b2_hi_ok"), sem("b2_lo_ok")
        q_in = [sem(f"q_in{k}") for k in range(KT)]
        q_diag, q_hi_ok, q_lo_ok = sem("q_diag"), sem("q_hi_ok"), sem("q_lo_ok")
        g_zero = sem("g_zero")
        x_ok, g_in, g_ok = sem("x_ok"), sem("g_in"), sem("g_ok")
        y_done, y_hi_ok, y_lo_ok = sem("y_done"), sem("y_hi_ok"), sem("y_lo_ok")
        v_done, low_ok = sem("v_done"), sem("low_ok")
        low_t_done, low_hi_ok, low_lo_ok = sem("low_t_done"), sem("low_hi_ok"), sem("low_lo_ok")
        lora_done, route, ex_ok, gated_ok = sem("lora_done"), sem("route"), sem("ex_ok"), sem("gated_ok")
        top_wait = sem("top_wait")
        gt_done, gt_hi_ok, gt_lo_ok = sem("gt_done"), sem("gt_hi_ok"), sem("gt_lo_ok")
        x3_done, x3n_ok = sem("x3_done"), sem("x3n_ok")
        x3t_done, x3t_hi_ok, x3t_lo_ok = sem("x3t_done"), sem("x3t_hi_ok"), sem("x3t_lo_ok")
        mask_ok = [sem(f"mask_ok{s}") for s in range(RING)]
        sign_even, sign_odd, slice_used = sem("sign_even"), sem("sign_odd"), sem("slice_used")
        last_in = [sem(f"last_in{k}") for k in range(KT)]
        p_half_used = sem("p_half_used")
        last_bias, last_m3 = sem("last_bias"), sem("last_m3")
        bias_in, out_step, out_ok, stored = sem("bias_in"), sem("out_step"), sem("out_ok"), sem("stored")

        x_v = x.rearrange("(n b) c f -> n (b c) f", b=2)
        out_v = out.rearrange("(n b) c (h f) -> n h (b c) f", b=2, h=2)
        mask_v = mask.rearrange("(n b) (k p) (h f) -> n h k p b f", b=2, p=P, h=2)
        bias_v = bias.rearrange("(h a f) -> h a f", h=2, a=1)
        w0_v = w0.rearrange("(k p) (i c) -> i p k c", p=P, c=P)
        m2_v = m2ext.rearrange("(k p) n -> k p n", p=P)
        w3_v = w3t.rearrange("(k p) n -> k p n", p=P)
        bw_v = bw.rearrange("(k p) r -> p k r", p=P)

        def pair_of(view, t):
            return view[bass.ds(t, 1)]

        def y_half(yh):
            return yt[:, 4 * yh:4 * yh + 4]

        def in4(ps):
            return ps[:, :].rearrange("p (k n) -> p k n", k=4)

        def pair_a(tile):
            return tile[:, :, NEXT:NPV].rearrange("p k (b r) -> p b k r", b=2)

        LAST_ON_DVE = (0, 2)
        LAST_ON_ACT = (1, 3, 4, 5, 6, 7)

        q_first = [0, 1]
        q_at = {0: [2], 5: [3], 7: [4], 10: [5], 12: [6, 7]}

        block = ctx.enter_context(nc.Block())

        @block.sync
        def _(sp):
            def load_x(t):
                sp.dma_start(x_in[:, :], pair_of(x_v, t).rearrange("a p f -> p (a f)")).then_inc(x_ok, 16)

            def load_g(t):
                for b in range(2):
                    c = sp.value_load(picks_sb[0:1, 0, bass.ds(2 * t + b, 1)], min_val=0, max_val=w1.shape[0] - 1)
                    sp.dma_start(g[TOK * b:TOK * b + TOK, TOK * b:TOK * b + TOK],
                                 w1[bass.ds(c, 1)].rearrange("a c d -> c (a d)")).then_inc(g_in, 16)

            def load_a(t):
                for b in range(2):
                    c = sp.value_load(picks_sb[0:1, 1, bass.ds(2 * t + b, 1)],
                                      min_val=0, max_val=labelers.shape[0] - 1)
                    sp.dma_start(a_raw[:, b, :, :].rearrange("p k r -> p (k r)"),
                                 labelers[bass.ds(c, 1)].rearrange("a p n -> p (a n)")).then_inc(a_in, 16)

            def load_mask(q, s):
                sp.dma_start(mask_in[:, s % RING, :, :],
                             pair_of(mask_v[:, s // KT, s % KT], q).rearrange("a p b f -> p (a b) f"))\
                    .then_inc(mask_ok[s % RING], 16)

            def load_last(k):
                sp.dma_start(last_mask[:, :, k, 0:HALF], mask_v[PAIRS - 1, 1, k])\
                    .then_inc(last_in[k], 16)

            def load_bias(half, out_sb=out_sb, signal=bias_in):
                sp.dma_start(out_sb[:, :], bias_v[half].to_broadcast([P, HALF])).then_inc(signal, 16)

            def store(q, half, out_sb=out_sb):
                sp.dma_start(pair_of(out_v[:, half], q).rearrange("a p f -> p (a f)"), out_sb[:, :])\
                    .then_inc(stored, 16)

            sp.dma_start(m0_raw[0][:, 0:FIRST, :], w0_v[0][:, 0:FIRST]).then_inc(first_in, 16)
            for k in range(KT):
                sp.dma_start(m2_raw[:, k, :], m2_v[k]).then_inc(m2_in[k], 16)
                if k == 0:
                    sp.dma_start(m0_raw[0][:, FIRST:, :], w0_v[0][:, FIRST:]).then_inc(m0_in[0], 16)
                elif k == 1:
                    sp.dma_start(m0_raw[1][:, :, :], w0_v[1]).then_inc(m0_in[1], 16)
            sp.dma_start(picks_sb[:, :, :], picks.rearrange("(a i) n -> a i n", a=1)).then_inc(tables_in, 16)
            sp.dma_start(lang_i[:, :], lang).then_inc(tables_in, 16)
            sp.dma_start(coeff_sb[:, :], coeff).then_inc(tables_in, 16)
            sp.dma_start(bw_raw[:, :, :], bw_v).then_inc(bw_in, 16)
            sp.dma_start(b2_raw[:, :], b2).then_inc(b2_in, 16)
            sp.wait_ge(tables_in, 48)
            load_a(0)
            load_x(0)
            with sp.Fori(1, KT // 2) as i2:
                for j in range(2):
                    sp.wait_ge(m0_used, 2 * i2 + j - 1)
                    sp.dma_start(m0_raw[j][:, :, :],
                                 pair_of(w0_v, 2 * i2 + j).rearrange("a p k c -> p (a k) c")).then_inc(m0_in[j], 16)
            sp.wait_ge(g_zero, 1)
            load_g(0)
            load_bias(0)
            for s in range(4):
                load_mask(0, s)
            for k in range(KT):
                sp.wait_ge(m2_used, k + 1)
                sp.dma_start(q_raw[:, k, :], w3_v[k]).then_inc(q_in[k], 16)
                if k == 5:
                    sp.wait_ge(y_done, 2)
                    load_x(1)
                    load_g(1)
            sp.wait_ge(a_lo_ok, 1)
            load_a(1)
            for s in range(4, RING):
                load_mask(0, s)

            def iteration(t, prefetch):
                q = t - 1
                for s in range(STEPS):
                    if s == 3 and prefetch:
                        sp.wait_ge(y_done, 2 * t + 2)
                        load_x(t + 1)
                        load_g(t + 1)
                        sp.wait_ge(a_lo_ok, t + 1)
                        load_a(t + 1)
                    sp.wait_ge(slice_used, STEPS * q + s + 1)
                    load_mask(q if s < STEPS - RING else q + 1, (s + RING) % STEPS)
                    if s == 4 and not prefetch:
                        sp.wait_ge(y_done, 2 * PAIRS)
                        load_bias(0, last_out[0], last_bias)
                        load_bias(1, last_out[1], last_bias)
                    if s in (8, 10) and not prefetch:
                        sp.wait_ge(p_half_used, PAIRS)
                        load_last((s - 8) // 2)
                    if s == 9:
                        sp.wait_ge(out_ok, 2 * q + 2)
                        store(q, 0)
                    if s == 11:
                        sp.wait_ge(stored, 16 * (2 * q + 1))
                        load_bias(1)
                if prefetch:
                    sp.wait_ge(out_ok, 2 * q + 3)
                    store(q, 1)
                    sp.wait_ge(stored, 16 * (2 * q + 2))
                    load_bias(0)

            with sp.Fori(1, PAIRS - 1) as t:
                iteration(t, True)
            iteration(PAIRS - 1, False)
            for k in range(2, KT):
                load_last(k)
            sp.wait_ge(out_ok, 2 * PAIRS - 1)
            store(PAIRS - 2, 1)
            sp.wait_ge(out_ok, 2 * PAIRS)
            store(PAIRS - 1, 0, last_out[0])
            quarter = HALF // 2
            for c in range(2):
                if c == 0:
                    sp.wait_ge(out_step, 8 * PAIRS + 1)
                else:
                    sp.wait_ge(out_ok, 2 * PAIRS + 1)
                cols = slice(quarter * c, quarter * c + quarter)
                sp.dma_start(out_v[PAIRS - 1, 1][:, cols], last_out[1][:, cols]).then_inc(stored, 16)
            sp.wait_ge(stored, 16 * (2 * PAIRS + 1))

        @block.gpsimd
        def _(pool):
            nc.gpsimd.memset(ident[:, :], 0.0).then_inc(ident_ok, 1)
            nc.gpsimd.memset(g[:, :], 0.0).then_inc(g_zero, 1)
            pool.wait_ge(ident_ok, 1)
            nc.gpsimd.affine_select(out=ident[:, :], in_=ident[:, :], compare_op=ALU.not_equal, fill=1.0,
                                    base=0, pattern=[[-1, P]], channel_multiplier=1).then_inc(ident_ok, 1)

        @block.scalar
        def _(act):
            def hi(dst, src, scale=1.0):
                return nc.scalar.activation(dst, src, ACT.Copy, scale=scale)

            act.wait_ge(first_diag, 1)
            hi(m0_hi[0][:, 0:FIRST, :], m0_raw[0][:, 0:FIRST, :]).then_inc(first_hi_ok, 1)
            for k in range(KT):
                act.wait_ge(m2_diag, k + 1)
                hi(m2_hi[:, k, :], m2_raw[:, k, :]).then_inc(m2_hi_ok, 1)
                if k == 0:
                    act.wait_ge(m0_in[0], 16)
                    hi(m0_hi[0][:, FIRST:, :], m0_raw[0][:, FIRST:, :]).then_inc(m0_hi_ok, 1)
                elif k == 1:
                    act.wait_ge(m0_diag, 1)
                    hi(m0_hi[1][:, :, :], m0_raw[1][:, :, :]).then_inc(m0_hi_ok, 1)

            def a_hi(t):
                act.wait_ge(a_in, 32 * (t + 1))
                if not (isinstance(t, int) and t == 0):
                    act.wait_ge(v_done, t)
                hi(pair_a(pv_hi), a_raw[:, :, :, :]).then_inc(a_hi_ok, 1)

            a_hi(0)
            act.wait_ge(b2_in, 16)
            hi(b2_hi[:, :], b2_raw[:, :]).then_inc(b2_hi_ok, 1)

            def p_hi(i, j):
                act.wait_ge(m0_used, i + 1)
                for c in range(3):
                    w = cuts[c + 1] - cuts[c]
                    dst = pv_hi[:, bass.ds(i, 1), cuts[c]:cuts[c + 1]].rearrange("p a n -> p (a n)")
                    hi(dst, set_ps[j][c][:, 0:w]).then_inc(p_hi_ok, 1)

            with act.Fori(0, KT // 2 - 1) as i2:
                for j in range(2):
                    p_hi(2 * i2 + j, j)
                    act.wait_ge(m0_diag, 2 * i2 + j + 2)
                    hi(m0_hi[j][:, :, :], m0_raw[j][:, :, :]).then_inc(m0_hi_ok, 1)
            p_hi(KT - 2, 0)
            act.wait_ge(bw_in, 16)
            for c in range(3):
                ins = hi(m0_hi[0][:, :, RL * c:RL * c + RL], bw_raw[:, :, :], scale=0.5)
            ins.then_inc(m0_hi_ok, 1)
            p_hi(KT - 1, 1)

            def y_hi(t, yh, ps):
                act.wait_ge(y_done, 2 * t + yh + 1)
                hi(y_half(yh)[:, :, 0, :], in4(ps)).then_inc(y_hi_ok, 1)

            def q_upper(k):
                act.wait_ge(q_diag, k + 1)
                hi(q_hi[:, k, :], q_raw[:, k, :]).then_inc(q_hi_ok, 1)

            def to_sign(q, s):
                act.wait_ge(mask_ok[s % RING], 16 * (2 * q + s // RING + 1))
                nc.scalar.activation(sign[:, s % RING, :, :], mask_in[:, s % RING, :, :], ACT.Copy,
                                     scale=2.0, bias=-1.0).then_inc(sign_odd, 1)

            for s in range(1, AHEAD, 2):
                to_sign(0, s)
            y_hi(0, 0, r2)
            y_hi(0, 1, r0)
            for k in q_first:
                q_upper(k)
            act.wait_ge(m2_used, KT)
            for c in range(3):
                w = cuts[c + 1] - cuts[c]
                hi(bs[:, cuts[c]:cuts[c + 1]], set_ps[0][c][:, 0:w]).then_inc(p_hi_ok, 1)

            def x3t_hi(t, h):
                act.wait_ge(x3t_done, 2 * t + h + 1)
                hi(x3t[:, 4 * h:4 * h + 4, 1:3, :],
                   r1[:, :].rearrange("p (k b n) -> p k b n", k=4, b=2)).then_inc(x3t_hi_ok, 1)

            def x3_out(t, h):
                act.wait_ge(x3_done, 2 * t + h + 1)
                if h == 0:
                    nc.scalar.activation(x3n[:, :], c_ps[0][:, :], ACT.Copy).then_inc(x3n_ok, 1)
                else:
                    act.wait_ge(x3t_done, 2 * t + 1)
                    nc.scalar.activation(x3n[:, 0:HALF - PX], c_ps[1][:, 0:HALF - PX], ACT.Copy)
                    nc.scalar.activation(x3n[:, HALF - PX:HALF], r0[:, 0:PX], ACT.Copy).then_inc(x3n_ok, 1)

            def iteration(t, back, prefetch):
                q = t - 1
                if back:
                    y_hi(t, 0, r2)
                    x3t_hi(q, 1)
                    y_hi(t, 1, r0)
                for s in range(STEPS):
                    if s == 15:
                        x3t_hi(t, 0)
                    if back and s % 2 == 1:
                        to_sign(q if s + AHEAD < STEPS else q + 1, (s + AHEAD) % STEPS)
                    if s == 6:
                        act.wait_ge(low_t_done, t + 1)
                        hi(low_t[:, :], r1[:, 0:P]).then_inc(low_hi_ok, 1)
                    if s == 9:
                        act.wait_ge(route, 11 * t + 2)
                        nc.scalar.activation(ex[:, :], top[:, 0:1], ACT.Exp, scale=-1.0, bias=top[:, 1:2])\
                            .then_inc(ex_ok, 1)
                    if s == 12:
                        act.wait_ge(gt_done, t + 1)
                        hi(gt_hi[:, :], r2[:, 0:P]).then_inc(gt_hi_ok, 1)
                    if s == 13:
                        x3_out(t, 0)
                    for k in q_at.get(s, []) if not back else []:
                        q_upper(k)
                    if prefetch and s == 12:
                        a_hi(t + 1)
                x3_out(t, 1)

            iteration(0, False, True)
            with act.Fori(1, PAIRS - 1) as t:
                iteration(t, True, True)
            iteration(PAIRS - 1, True, False)
            to_sign(PAIRS - 1, 5)
            x3t_hi(PAIRS - 1, 1)
            to_sign(PAIRS - 1, 7)
            for k in LAST_ON_ACT:
                act.wait_ge(last_in[k], 16)
                nc.scalar.activation(last_sign[:, :, k, 0:HALF], last_mask[:, :, k, 0:HALF], ACT.Copy,
                                     scale=2.0, bias=-1.0).then_inc(sign_odd, 1)

        @block.vector
        def _(dve):
            def lo(dst, src, hi_part):
                return nc.vector.tensor_tensor(dst, src, hi_part.bitcast(F32), ALU.subtract)

            def add_diag(tile):
                return nc.vector.tensor_tensor(tile, tile, ident[:, :], ALU.add)

            dve.sem_inc(out_ok, 1)
            dve.wait_ge(ident_ok, 2)

            def m0_lower(i, tiles=slice(0, KT)):
                dve.wait_ge(m0_hi_ok, i + 1)
                lo(m0_lo[i][:, tiles, :], m0_raw[i][:, tiles, :], m0_hi[i][:, tiles, :]).then_inc(m0_lo_ok, 1)

            def m2_diagonal(k):
                dve.wait_ge(m2_in[k], 16)
                add_diag(m2_raw[:, k, P * k:P * k + P]).then_inc(m2_diag, 1)

            dve.wait_ge(first_in, 16)
            add_diag(m0_raw[0][:, 0, :]).then_inc(first_diag, 1)
            dve.wait_ge(first_hi_ok, 1)
            lo(m0_lo[0][:, 0:FIRST, :], m0_raw[0][:, 0:FIRST, :], m0_hi[0][:, 0:FIRST, :]).then_inc(first_lo_ok, 1)
            m2_diagonal(0)
            for k in range(KT):
                if 2 <= k < KT - 1:
                    m2_diagonal(k + 1)
                dve.wait_ge(m2_hi_ok, k + 1)
                lo(m2_lo[:, k, :], m2_raw[:, k, :], m2_hi[:, k, :]).then_inc(m2_lo_ok, 1)
                if k < 2:
                    m2_diagonal(k + 1)
                if k == 0:
                    m0_lower(0, slice(FIRST, KT))
                    dve.wait_ge(m0_in[1], 16)
                    add_diag(m0_raw[1][:, 1, :]).then_inc(m0_diag, 1)
                elif k == 1:
                    m0_lower(1)

            def a_lo(t):
                dve.wait_ge(a_hi_ok, t + 1)
                lo(pair_a(pv_lo), a_raw[:, :, :, :], pair_a(pv_hi)).then_inc(a_lo_ok, 1)

            a_lo(0)
            dve.wait_ge(b2_hi_ok, 1)
            lo(b2_lo[:, :], b2_raw[:, :], b2_hi[:, :]).then_inc(b2_lo_ok, 1)

            dve.wait_ge(tables_in, 48)
            nc.vector.tensor_copy(lang_f[:, :], lang_i[:, :]).then_inc(tables_ok, 1)
            for e in range(E):
                nc.vector.memset(iota[:, e:e + 1], float(e)).then_inc(tables_ok, 1)
            dve.wait_ge(tables_ok, 1)
            for e in range(E):
                nc.vector.tensor_scalar(lang_hot[:, :, e], lang_f[:, :], float(e), LANG_BIAS,
                                        ALU.is_equal, ALU.mult).then_inc(tables_ok, 1)
            TABLES = 1 + 2 * E

            def p_lo(i, j):
                for c in range(3):
                    w = cuts[c + 1] - cuts[c]
                    dve.wait_ge(p_hi_ok, 3 * i + c + 1)
                    at_lo = pv_lo[:, bass.ds(i, 1), cuts[c]:cuts[c + 1]].rearrange("p a n -> p (a n)")
                    at_hi = pv_hi[:, bass.ds(i, 1), cuts[c]:cuts[c + 1]].rearrange("p a n -> p (a n)")
                    lo(at_lo, set_ps[j][c][:, 0:w], at_hi).then_inc(p_lo_ok, 1)

            with dve.Fori(0, KT // 2 - 1) as i2:
                for j in range(2):
                    p_lo(2 * i2 + j, j)
                    dve.wait_ge(m0_in[j], 16 * (i2 + 2))
                    add_diag(m0_raw[j][:, bass.ds(2 * i2 + j + 2, 1), :].rearrange("p a n -> p (a n)"))\
                        .then_inc(m0_diag, 1)
                    dve.wait_ge(m0_hi_ok, 2 * i2 + j + 3)
                    lo(m0_lo[j][:, :, :], m0_raw[j][:, :, :], m0_hi[j][:, :, :]).then_inc(m0_lo_ok, 1)
            p_lo(KT - 2, 0)
            dve.wait_ge(m0_hi_ok, KT + 1)
            nc.vector.scalar_tensor_tensor(out=m0_hi[0][:, :, 3 * RL:], in0=bw_raw[:, :, :], scalar=0.5,
                                           in1=m0_hi[0][:, :, 0:RL].bitcast(F32),
                                           op0=ALU.mult, op1=ALU.subtract).then_inc(m0_lo_ok, 1)

            def make_g(t):
                dve.wait_ge(g_in, 32 * (t + 1))
                add_diag(g[:, :]).then_inc(g_ok, 1)

            def y_lo(t, yh, ps):
                dve.wait_ge(y_hi_ok, 2 * t + yh + 1)
                lo(y_half(yh)[:, :, 1, :], in4(ps), y_half(yh)[:, :, 0, :]).then_inc(y_lo_ok, 1)

            dve.wait_ge(tables_ok, TABLES)
            make_g(0)
            p_lo(KT - 1, 1)

            def to_sign(q, s):
                dve.wait_ge(mask_ok[s % RING], 16 * (2 * q + s // RING + 1))
                nc.vector.tensor_scalar(sign[:, s % RING, :, :], mask_in[:, s % RING, :, :], 2.0, -1.0,
                                        ALU.mult, ALU.add).then_inc(sign_even, 1)

            def q_diagonal(k):
                dve.wait_ge(q_in[k], 16)
                add_diag(q_raw[:, k, P * k:P * k + P]).then_inc(q_diag, 1)

            def q_lower(k):
                if k + 1 < KT:
                    q_diagonal(k + 1)
                dve.wait_ge(q_hi_ok, k + 1)
                lo(q_lo[:, k, :], q_raw[:, k, :], q_hi[:, k, :]).then_inc(q_lo_ok, 1)

            for s in range(0, AHEAD, 2):
                to_sign(0, s)
            y_lo(0, 0, r2)
            y_lo(0, 1, r0)
            q_diagonal(0)
            for k in q_first:
                q_lower(k)
            for c in range(3):
                w = cuts[c + 1] - cuts[c]
                dve.wait_ge(p_hi_ok, 3 * KT + c + 1)
                rows = bs[RL:2 * RL, cuts[c]:cuts[c + 1]]
                lo(rows, set_ps[0][c][RL:2 * RL, 0:w], rows).then_inc(p_lo_ok, 1)

            def x3t_lo(t, h):
                dve.wait_ge(x3t_hi_ok, 2 * t + h + 1)
                tiles = slice(4 * h, 4 * h + 4)
                ps = r1[:, :].rearrange("p (k b n) -> p k b n", k=4, b=2)
                lo(x3t[:, tiles, 0:4:3, :], ps, x3t[:, tiles, 1:3, :])
                lo(x3t[:, tiles, 4:6, :], ps, x3t[:, tiles, 1:3, :]).then_inc(x3t_lo_ok, 1)

            def pick_low(t):
                dve.wait_ge(v_done, t + 1)
                for b in range(2):
                    mine = slice(TOK * b, TOK * b + TOK)
                    cols = r0[mine, LOW0 + RL * b:LOW0 + RL * b + RL]
                    nc.vector.tensor_copy(low[mine, :, :], cols.unsqueeze(1).to_broadcast([TOK, 4, RL]))\
                        .then_inc(low_ok, 1)

            def route_top(t):
                dve.wait_ge(lora_done, t + 1)
                nc.vector.tensor_tensor(logits[:, :], r0[:, PX:A0],
                                        lang_hot[:, bass.ds(t, 1), :].rearrange("p a e -> p (a e)"), ALU.add)\
                    .then_inc(route, 1)
                dve.wait_ge(route, 11 * t + 1).then_inc(top_wait, 1)
                nc.vector.max(top[:, :], logits[:, :]).then_inc(route, 1)
                dve.wait_ge(route, 11 * t + 2).then_inc(top_wait, 1)
                nc.vector.max_index(top_at[:, :], top[:, :], logits[:, :]).then_inc(route, 1)
                dve.wait_ge(route, 11 * t + 3)
                nc.vector.tensor_copy(top_f[:, :], top_at[:, 0:2]).then_inc(route, 1)

            def route_gates(t):
                dve.wait_ge(ex_ok, t + 1)
                nc.vector.tensor_scalar(den[:, :], ex[:, :], 1.0, None, ALU.add).then_inc(route, 1)
                dve.wait_ge(route, 11 * t + 5)
                nc.vector.reciprocal(rden[:, :], den[:, :]).then_inc(route, 1)
                dve.wait_ge(route, 11 * t + 6)
                nc.vector.tensor_scalar(w_a[:, :], rden[:, :], 2.0, None, ALU.mult).then_inc(route, 1)
                nc.vector.tensor_scalar(w_b[:, :], rden[:, :], ex[:, 0:1], 2.0, ALU.mult, ALU.mult)\
                    .then_inc(route, 1)
                dve.wait_ge(route, 11 * t + 8)
                nc.vector.tensor_scalar(gate_a[:, :], iota[:, :], top_f[:, 0:1], w_a[:, 0:1],
                                        ALU.is_equal, ALU.mult).then_inc(route, 1)
                nc.vector.tensor_scalar(gate_b[:, :], iota[:, :], top_f[:, 1:2], w_b[:, 0:1],
                                        ALU.is_equal, ALU.mult).then_inc(route, 1)
                dve.wait_ge(route, 11 * t + 10)
                nc.vector.tensor_tensor(gates[:, :], gate_a[:, :], gate_b[:, :], ALU.add).then_inc(route, 1)
                dve.wait_ge(route, 11 * t + 11)
                nc.vector.tensor_tensor(gated[:, :, :], r0[:, A0:LOW0].rearrange("p (e r) -> p e r", e=E),
                                        gates[:, :].unsqueeze(2).to_broadcast([P, E, R]), ALU.mult)\
                    .then_inc(gated_ok, 1)

            def finish_half(q, h, banks, out_sb, last=False):
                n = 4 * (2 * q + h)
                dve.wait_ge(slice_used, STEPS * q + KT * (h + 1))
                if last:
                    dve.wait_ge(last_bias, 32)
                else:
                    dve.wait_ge(bias_in, 16 * (2 * q + h + 1))
                nc.vector.tensor_tensor(out_sb[:, :], banks[0][:, :], out_sb[:, :], ALU.add).then_inc(out_step, 1)
                for part in range(2):
                    for b, ps in enumerate(banks[1:]):
                        mine = slice(TOK * b, TOK * b + TOK)
                        if b == 0:
                            dve.wait_ge(out_step, n + (1 if part == 0 else 2))
                        elif part == 1:
                            dve.wait_ge(out_step, n + 3)
                        ins = nc.vector.scalar_tensor_tensor(
                            out=out_sb[mine, :], in0=ps[TOK * part:TOK * part + TOK, :],
                            scalar=coeff_sb[mine, bass.ds(q, 1)], in1=out_sb[mine, :],
                            op0=ALU.mult, op1=ALU.add)
                        if part == 1 and b == 1:
                            ins.then_inc(out_ok, 1)
                        else:
                            ins.then_inc(out_step, 1)

            def iteration(t, back, prefetch):
                q = t - 1
                if back:
                    y_lo(t, 0, r2)
                    y_lo(t, 1, r0)
                    x3t_lo(q, 1)
                for s in range(STEPS):
                    if back and s % 2 == 0:
                        to_sign(q if s + AHEAD < STEPS else q + 1, (s + AHEAD) % STEPS)
                    if s == 4:
                        pick_low(t)
                    if s == 6:
                        dve.wait_ge(low_hi_ok, t + 1)
                        rows = low_t[2 * RL:3 * RL, :]
                        lo(rows, r1[2 * RL:3 * RL, 0:P], rows).then_inc(low_lo_ok, 1)
                    if back and s == 7:
                        finish_half(q, 0, back_ps, out_sb)
                    if s == 8:
                        route_top(t)
                    if s == 9:
                        route_gates(t)
                    if s == 12:
                        dve.wait_ge(gt_hi_ok, t + 1)
                        lo(gt_lo[:, :], r2[:, 0:P], gt_hi[:, :]).then_inc(gt_lo_ok, 1)
                    if prefetch and s == 13:
                        make_g(t + 1)
                    if s == 15:
                        x3t_lo(t, 0)
                    for k in q_at.get(s, []) if not back else []:
                        q_lower(k)
                    if prefetch and s == 12:
                        a_lo(t + 1)
                if back:
                    finish_half(q, 1, back_ps, out_sb)

            iteration(0, False, True)
            with dve.Fori(1, PAIRS - 1) as t:
                iteration(t, True, True)
            iteration(PAIRS - 1, True, False)
            q = PAIRS - 1
            to_sign(q, 4)
            x3t_lo(q, 1)
            to_sign(q, 6)
            for k in LAST_ON_DVE:
                dve.wait_ge(last_in[k], 16)
                nc.vector.tensor_scalar(last_sign[:, :, k, 0:HALF], last_mask[:, :, k, 0:HALF], 2.0, -1.0,
                                        ALU.mult, ALU.add).then_inc(sign_even, 1)
            finish_half(q, 0, spare_ps, last_out[0], True)

            done = last_out[1]
            steps = 4 * (2 * q + 1)
            dve.wait_ge(last_m3, 1)
            cols = slice(0, HALF // 2)
            nc.vector.tensor_tensor(done[:, cols], back_ps[0][:, cols], done[:, cols], ALU.add).then_inc(out_step, 1)
            dve.wait_ge(slice_used, STEPS * PAIRS)
            for part in range(2):
                for b, ps in enumerate(back_ps[1:]):
                    mine = slice(TOK * b, TOK * b + TOK)
                    dve.wait_ge(out_step, steps + (1 if part == 0 else 2 + b))
                    nc.vector.scalar_tensor_tensor(
                        out=done[mine, :], in0=ps[TOK * part:TOK * part + TOK, :], scalar=coeff_sb[mine, q:q + 1],
                        in1=done[mine, :], op0=ALU.mult, op1=ALU.add).then_inc(out_step, 1)
            dve.wait_ge(out_step, steps + 5)
            dve.wait_ge(last_m3, 2)
            nc.vector.tensor_tensor(done[:, HALF // 2:], c_ps[1][:, 0:HALF // 2], done[:, HALF // 2:], ALU.add)\
                .then_inc(out_ok, 1)

        @block.tensor
        def _(pe):
            mm = nc.tensor.matmul

            def setup_step(j, k, arriving=False):
                hi_t, lo_t = m0_hi[j], m0_lo[j]
                for n, (a, b) in enumerate(((hi_t, m2_hi), (lo_t, m2_hi), (hi_t, m2_lo))):
                    first = j == 0 and k < FIRST
                    if arriving and n == 0:
                        pe.wait_ge(first_hi_ok if first else m0_hi_ok, j + 1)
                        pe.wait_ge(m2_hi_ok, k + 1)
                    elif arriving and n == 1:
                        pe.wait_ge(first_lo_ok if first else m0_lo_ok, j + 1)
                    elif arriving:
                        pe.wait_ge(m2_lo_ok, k + 1)
                    for c in range(3):
                        w = cuts[c + 1] - cuts[c]
                        ins = mm(set_ps[j][c][:, 0:w], a[:, k, :], b[:, k, cuts[c]:cuts[c + 1]],
                                 start=(k == 0 and n == 0), stop=(k == KT - 1 and n == 2))
                if k == KT - 1:
                    ins.then_inc(m0_used, 1)

            ahead = iter(range(KT))
            for k in range(KT):
                setup_step(0, k, True)
                if k % 2 == 1:
                    setup_step(1, next(ahead), True)
            for k in ahead:
                setup_step(1, k, True)
            with pe.Fori(1, KT // 2) as i2:
                for j in range(2):
                    pe.wait_ge(m0_lo_ok, 2 * i2 + j + 1)
                    pe.wait_ge(p_lo_ok, 3 * (2 * i2 + j - 1))
                    for k in range(KT):
                        setup_step(j, k)

            def low_rank_step(k):
                for c in range(3):
                    w = cuts[c + 1] - cuts[c]
                    mm(set_ps[0][c][:, 0:w], m0_hi[0][:, k, :], m2_hi[:, k, cuts[c]:cuts[c + 1]],
                       start=(k == 0), stop=(k == KT - 1), skip_group_check=True)
                for c in range(3):
                    w = cuts[c + 1] - cuts[c]
                    ins = mm(set_ps[0][c][0:3 * RL, 0:w], m0_hi[0][:, k, 0:3 * RL],
                             m2_lo[:, k, cuts[c]:cuts[c + 1]], start=False, stop=(k == KT - 1),
                             skip_group_check=True)
                ins.then_inc(m2_used, 1)

            def y_part(t, yh, ps):
                if yh == 0:
                    pe.wait_ge(x_ok, 16 * (t + 1))
                    pe.wait_ge(g_ok, t + 1)
                for k in range(4):
                    n = P * (4 * yh + k)
                    ins = mm(ps[:, P * k:P * k + P], x_in[:, n:n + P], g[:, :], start=True, stop=True)
                ins.then_inc(y_done, 1)

            def v_step(t, k):
                if k == 0:
                    pe.wait_ge(y_lo_ok, 2 * t + 2)
                    pe.wait_ge(a_lo_ok, t + 1)
                for n, (a, b) in enumerate(((0, pv_hi), (0, pv_lo), (1, pv_hi))):
                    ins = mm(r0[:, 0:NV], yt[:, k, a, :], b[:, k, V0:NPV],
                             start=(k == 0 and n == 0), stop=(k == KT - 1 and n == 2), skip_group_check=True)
                if k == KT - 1:
                    ins.then_inc(v_done, 1)

            def low_turn(t):
                pe.wait_ge(low_ok, 2 * t + 2)
                if not (isinstance(t, int) and t == 0):
                    pe.wait_ge(x3t_lo_ok, 2 * t)
                nc.tensor.transpose(r1[:, 0:P], low[:, :, :].rearrange("p c r -> p (c r)"), ident[:, :])\
                    .then_inc(low_t_done, 1)

            def lora(t):
                pe.wait_ge(low_lo_ok, t + 1)
                mm(r0[:, 0:LOW0], low_t[:, :], bs[:, V0:NEXT], start=False, stop=True,
                   skip_group_check=True).then_inc(lora_done, 1)

            def x3_step(t, h, k):
                cols = slice(HALF * h, min(HALF * h + HALF, V0))
                n_cols = cols.stop - cols.start
                if isinstance(t, int) and t == 0 and k == 0:
                    pe.wait_ge(p_lo_ok, 3 * (KT + 1))
                for n, (a, b) in enumerate(((0, pv_hi), (0, pv_lo), (1, pv_hi))):
                    ins = mm(c_ps[h][:, 0:n_cols], yt[:, k, a, :], b[:, k, cols],
                             start=(k == 0 and n == 0), stop=False)
                if h == 0 and k == KT - 1:
                    ins.then_inc(p_half_used, 1)

            def x3_tail(t, h):
                pe.wait_ge(gt_lo_ok, t + 1)
                gated_passes = ((gt_hi, b2_hi), (gt_hi, b2_lo), (gt_lo, b2_hi))
                if h == 1:
                    for n, (a, b) in enumerate(gated_passes):
                        mm(r0[:, 0:PX], a[:, :], b[:, V0:D], start=False, stop=(n == 2), skip_group_check=True)
                cols = slice(HALF * h, min(HALF * h + HALF, V0))
                ps = c_ps[h][:, 0:cols.stop - cols.start]
                mm(ps, low_t[:, :], bs[:, cols], start=False, stop=False)
                for n, (a, b) in enumerate(gated_passes):
                    ins = mm(ps, a[:, :], b[:, cols], start=False, stop=(n == 2))
                ins.then_inc(x3_done, 1)

            def turn_gated(t):
                pe.wait_ge(gated_ok, t + 1)
                nc.tensor.transpose(r2[:, 0:P], gated[:, :, :].rearrange("p e r -> p (e r)"), ident[:, :])\
                    .then_inc(gt_done, 1)

            def turn_x3(t, h):
                pe.wait_ge(x3n_ok, 2 * t + h + 1)
                if h == 1:
                    pe.wait_ge(x3t_lo_ok, 2 * t + 1)
                for k in range(4):
                    ins = nc.tensor.transpose(r1[:, P * k:P * k + P], x3n[:, P * k:P * k + P], ident[:, :])
                ins.then_inc(x3t_done, 1)

            def m3_step(k, ps, cols):
                for n, (a, b) in enumerate(((1, q_hi), (1, q_lo), (4, q_hi))):
                    ins = mm(ps, x3t[:, k, a:a + 2, :].rearrange("p b n -> p (b n)"), b[:, k, cols],
                             start=(k == 0 and n == 0), stop=(k == KT - 1 and n == 2))
                return ins

            def sign_step(k, banks, signs, to_r0=False):
                for b, ps in enumerate(banks[1:]):
                    if to_r0 and b == 1:
                        pe.wait_ge(x3n_ok, 2 * PAIRS)
                    ins = mm(ps[:, :], x3t[:, k, 2 * b:2 * b + 2, :].rearrange("p l n -> p (l n)"), signs[:, b, :],
                             start=(k == 0), stop=(k == KT - 1))
                ins.then_inc(slice_used, 1)

            def last_half(q):
                pe.wait_ge(out_ok, 2 * q + 1)
                for c, ps in enumerate((back_ps[0], c_ps[1])):
                    for k in range(4 * c, 4 * c + 4):
                        if k in LAST_ON_DVE:
                            pe.wait_ge(sign_even, STEPS // 2 * q + KT // 2 + k // 2 + 1)
                        else:
                            pe.wait_ge(sign_odd, STEPS // 2 * q + KT // 2 + LAST_ON_ACT.index(k) + 1)
                        sign_step(k, back_ps, last_sign[:, :, k, 0:HALF])
                    for k in range(KT):
                        ins = m3_step(k, ps[:, 0:HALF // 2], slice(HALF + HALF // 2 * c, HALF + HALF // 2 * (c + 1)))
                    ins.then_inc(last_m3, 1)

            def back_step(q, s, banks):
                h, k = s // KT, s % KT
                cols = slice(HALF * h, HALF * h + HALF)
                if s == 0 and banks is back_ps:
                    pe.wait_ge(out_ok, 2 * q + 1)
                elif s == KT:
                    pe.wait_ge(out_ok, 2 * q + 2)
                if s == 0 or s == 4:
                    pe.wait_ge(x3t_lo_ok, 2 * q + s // 4 + 1)
                m3_step(k, banks[0][:, :], cols)
                pe.wait_ge(sign_even if s % 2 == 0 else sign_odd, STEPS // 2 * q + s // 2 + 1)
                sign_step(k, banks, sign[:, s % RING], s == 0 and banks is spare_ps)

            fill = [
                [], [("v", 0), ("v", 1), ("v", 2)], [("v", 3), ("v", 4), ("v", 5)], [("v", 6), ("v", 7)],
                [("x3", 0, 0)], [("low",), ("x3", 0, 1)], [("x3", 0, 2)],
                [("lora",), ("x3", 0, 3), ("x3", 0, 4), ("x3", 0, 5), ("x3", 0, 6), ("x3", 0, 7), ("x3", 1, 0)],
                [("x3", 1, 1)], [("x3", 1, 2)], [("x3", 1, 3)], [("gated",), ("x3", 1, 4)],
                [("tail", 0)], [("x3", 1, 5)], [("turn", 0)], [("x3", 1, 6), ("x3", 1, 7), ("tail", 1)],
            ]
            alone = [("v", k) for k in range(KT)] + [("x3", 0, k) for k in range(3)] + [("low",)]
            alone += [("x3", 0, k) for k in range(3, 6)] + [("lora",), ("x3", 0, 6), ("x3", 0, 7)]
            alone += [("x3", 1, k) for k in range(5)] + [("gated",), ("x3", 1, 5), ("tail", 0), ("x3", 1, 6)]
            alone += [("x3", 1, 7), ("turn", 0), ("tail", 1)]

            def front_work(t, item):
                kind = item[0]
                if kind == "v":
                    v_step(t, item[1])
                elif kind == "low":
                    low_turn(t)
                elif kind == "lora":
                    lora(t)
                elif kind == "x3":
                    x3_step(t, item[1], item[2])
                elif kind == "gated":
                    turn_gated(t)
                elif kind == "tail":
                    x3_tail(t, item[1])
                else:
                    turn_x3(t, item[1])

            def iteration(t, front):
                q = t - 1
                if front:
                    y_part(t, 0, r2)
                    turn_x3(q, 1)
                    y_part(t, 1, r0)
                for s in range(STEPS if front else KT):
                    back_step(q, s, back_ps if front else spare_ps)
                    if front:
                        for item in fill[s]:
                            front_work(t, item)
                    elif s == 1:
                        turn_x3(q, 1)
                if not front:
                    last_half(q)

            pe.wait_ge(m0_lo_ok, KT + 1)
            pe.wait_ge(p_lo_ok, 3 * (KT - 1))
            for k in range(KT):
                low_rank_step(k)
                if k == 3:
                    pe.wait_ge(ident_ok, 2)
                    pe.wait_ge(p_lo_ok, 3 * KT)
                    y_part(0, 0, r2)
                    y_part(0, 1, r0)
            pe.wait_ge(b2_lo_ok, 1)
            for item in alone:
                front_work(0, item)
            pe.wait_ge(q_lo_ok, KT)
            with pe.Fori(1, PAIRS) as t:
                iteration(t, True)
            iteration(PAIRS, False)


def kernel(**inputs):
    import numpy as np
    import concourse.bacc as bacc
    from concourse.bass_utils import run_bass_kernel_spmd

    def arr(name):
        return np.asarray(inputs[name])

    x = arr("x")
    pairs = x.shape[0] // 2

    def per_token(a):
        return np.repeat(a.reshape(pairs, 2).T, 64, axis=0)

    expert_a = arr("L2_cond_A")
    expert_b = arr("L2_cond_B")
    labeler_a = arr("L0_cond_lora_A")
    nl, d, rank = labeler_a.shape
    arrays = {
        "x": x,
        "picks": np.stack([arr("itok_B_0_15"), arr("itok_B_0_2")]),
        "lang": per_token(arr("itok_B_0_7")),
        "coeff": per_token(arr("condB_coeff")),
        "mask": arr("mask_Bx4096x4096_ik1"),
        "w0": arr("L0_cond_W"),
        "bw": arr("L0_cond_lora_B_w"),
        "labelers": labeler_a.reshape(nl, d // 128, 128, rank).transpose(0, 2, 1, 3).reshape(nl, 128, -1),
        "m2ext": np.concatenate([arr("L2_cond_W").T, arr("L2_cond_Wr").T, expert_a.reshape(-1, d).T], axis=1),
        "b2": expert_b.transpose(0, 2, 1).reshape(-1, d),
        "w3t": arr("L3_cond_W").T,
        "w1": arr("L1_cond_weights"),
        "bias": arr("L3_cond_b"),
    }
    nc = bacc.Bacc("TRN2", target_bir_lowering=False, num_devices=1, dynamic_dma_scratch_size=SCRATCH)
    feed, args = {}, {}
    for name, a in arrays.items():
        a = np.ascontiguousarray(a)
        feed[f"in_{name}"] = a
        args[name] = nc.dram_tensor(f"in_{name}", a.shape, mybir.dt.from_np(a.dtype), kind="ExternalInput").ap()
    args["out"] = nc.dram_tensor("out_x", x.shape, F32, kind="ExternalOutput").ap()
    layers_kernel(nc, **args)
    result = run_bass_kernel_spmd(nc, [feed], core_ids=[0])
    return result.results[0]["out_x"]
```
